# Optimizing a Trainium2 kernel written in Bass

```python
import numpy as np
import jax
import jax.numpy as jnp

def _softmax(x, axis=-1):
    return jax.nn.softmax(x, axis=axis)

def _gelu(x):
    return jax.nn.gelu(x, approximate=True)

def _silu(x):
    return jax.nn.silu(x)

def _sigmoid(x):
    return jax.nn.sigmoid(x)

def _layernorm(x, axis=-1, eps=1e-05):
    m = jnp.mean(x, axis=axis, keepdims=True)
    v = jnp.var(x, axis=axis, keepdims=True)
    return (x - m) / jnp.sqrt(v + eps)

def _scatter_add(tgt, idx, src, axis=0):
    return tgt.at[idx].add(src)

def _segment_sum(src, seg, n):
    return jax.ops.segment_sum(src, seg, n)
kernel_name = 'mk_decoder_postln_d2_seqx_r4_00c96a'

def setup_inputs(seed: int=0):
    np.random.seed(seed)
    _w = jnp.asarray

    def _rec_inputs():
        import jax
        import jax.numpy as jnp
        _rk = jax.random.key(seed)
        x = -0.0005207 + 1.001 * jax.random.normal(jax.random.fold_in(_rk, 1), (16, 256, 256), jnp.float32)
        _lenS = 256 - jax.random.randint(jax.random.fold_in(_rk, 7), (16,), 0, max(1, 256 // 4) + 1, jnp.int32)
        _lenS2 = 256 - jax.random.randint(jax.random.fold_in(_rk, 8), (16,), 0, max(1, 256 // 4) + 1, jnp.int32)
        _ctx_1024P = jax.random.normal(jax.random.fold_in(_rk, 11), (16, 16, 256), jnp.float32)
        _ctx_1024c = jax.random.dirichlet(jax.random.fold_in(_rk, 511), 0.3 * jnp.ones((16,), jnp.float32), (16, 256))
        _ctx_1024t = jnp.einsum('bsk,bkd->bsd', _ctx_1024c, _ctx_1024P)
        _ctx_1024t = _ctx_1024t * jax.lax.rsqrt(jnp.mean(jnp.square(_ctx_1024t)) + 1e-12) * 0.953939
        ctx_1024 = -1.39393e-06 + 0.999914 * (_ctx_1024t + 0.3 * jax.random.normal(jax.random.fold_in(_rk, 611), (16, 256, 256), jnp.float32))
        itok_BxSx64_0_2047 = jax.random.randint(jax.random.fold_in(_rk, 12), (16, 256, 64), 0, 512, jnp.int32)
        return (x, ctx_1024, itok_BxSx64_0_2047)
    x, ctx_1024, itok_BxSx64_0_2047 = _rec_inputs()

    def _L0_attn_setup():
        import jax, jax.numpy as jnp
        import numpy as np
        from jax import lax
        B, L, DM = (4, 1024, 256)
        D_INNER, D_STATE, D_CONV, DT_RANK = (512, 16, 4, 64)

        def _silu(v):
            return v * jax.nn.sigmoid(v)

        def _causal_depthwise_conv(xc, conv_w, conv_b):
            k = conv_w[:, None, :]
            y = lax.conv_general_dilated(xc, k, window_strides=(1,), padding=[(D_CONV - 1, 0)], dimension_numbers=('NCH', 'OIH', 'NCH'), feature_group_count=D_INNER)
            return y + conv_b[None, :, None]

        def _mamba_forward(x, W_in, conv_w, conv_b, W_xproj, W_dt, b_dt, A_log, Dp, W_out):
            xz = jnp.einsum('bld,de->ble', x, W_in)
            xin, z = jnp.split(xz, 2, axis=-1)
            xc = _causal_depthwise_conv(xin.transpose(0, 2, 1), conv_w, conv_b)
            xc = _silu(xc).transpose(0, 2, 1)
            x_dbl = jnp.einsum('bld,de->ble', xc, W_xproj)
            dt, Bm, Cm = jnp.split(x_dbl, [DT_RANK, DT_RANK + D_STATE], axis=-1)
            dt = jax.nn.softplus(jnp.einsum('blr,rd->bld', dt, W_dt) + b_dt)
            A = -jnp.exp(A_log)

            def step(h, inp):
                dt_t, B_t, C_t, x_t = inp
                dA = jnp.exp(dt_t[..., None] * A)
                dBx = dt_t[..., None] * B_t[:, None, :] * x_t[..., None]
                h = dA * h + dBx
                y_t = jnp.sum(h * C_t[:, None, :], axis=-1)
                return (h, y_t)
            h0 = jnp.zeros((x.shape[0], D_INNER, D_STATE), x.dtype)
            xs = (dt.transpose(1, 0, 2), Bm.transpose(1, 0, 2), Cm.transpose(1, 0, 2), xc.transpose(1, 0, 2))
            _, ys = lax.scan(step, h0, xs)
            y = ys.transpose(1, 0, 2) + xc * Dp
            y = y * _silu(z)
            return jnp.einsum('bld,de->ble', y, W_out)
        key = jax.random.key(seed)
        ks = jax.random.split(key, 8)
        s = 0.02
        x = jax.random.normal(ks[0], (B, L, DM), jnp.float32)
        W_in = jax.random.normal(ks[1], (DM, 2 * D_INNER), jnp.float32) * s
        conv_w = jax.random.normal(ks[2], (D_INNER, D_CONV), jnp.float32) * s
        conv_b = jnp.zeros((D_INNER,), jnp.float32)
        W_xproj = jax.random.normal(ks[3], (D_INNER, DT_RANK + 2 * D_STATE), jnp.float32) * s
        W_dt = jax.random.normal(ks[4], (DT_RANK, D_INNER), jnp.float32) * s
        b_dt = jnp.full((D_INNER,), -4.6, jnp.float32)
        A_log = jnp.log(jnp.broadcast_to(jnp.arange(1, D_STATE + 1, dtype=jnp.float32), (D_INNER, D_STATE)))
        Dp = jnp.ones((D_INNER,), jnp.float32)
        W_out = jax.random.normal(ks[5], (D_INNER, DM), jnp.float32) * s
        return {'x': x, 'W_in': W_in, 'conv_w': conv_w, 'conv_b': conv_b, 'W_xproj': W_xproj, 'W_dt': W_dt, 'b_dt': b_dt, 'A_log': A_log, 'Dp': Dp, 'W_out': W_out}
    _L0_attn_all = _L0_attn_setup()
    _L0_attn_in = {k: v for k, v in _L0_attn_all.items() if k in ('W_in', 'conv_w', 'conv_b', 'W_xproj', 'W_dt', 'b_dt', 'A_log', 'Dp', 'W_out')}
    del _L0_attn_all

    def _L0_xattn_setup():
        import jax, jax.numpy as jnp
        import numpy as np
        B, NQ, NKV, K = (2, 256, 512, 64)
        D, H, LAT = (256, 16, 128)
        HD = D // H
        SCALE = 1.0 / np.sqrt(HD)
        key = jax.random.key(seed)
        ks = jax.random.split(key, 7)
        s = lambda fan_in: 1.0 / np.sqrt(fan_in)
        return {'x_q': jax.random.normal(ks[0], (B, NQ, D), jnp.float32), 'x_kv': jax.random.normal(ks[1], (B, NKV, D), jnp.float32), 'indices': jax.random.randint(ks[2], (B, NQ, K), 0, NKV), 'W_q': jax.random.normal(ks[3], (D, D), jnp.float32) * s(D), 'W_kv_down': jax.random.normal(ks[4], (LAT, D), jnp.float32) * s(D), 'W_kv_up': jax.random.normal(ks[5], (2 * D, LAT), jnp.float32) * s(LAT), 'W_out': jax.random.normal(ks[6], (D, D), jnp.float32) * s(D)}
    _L0_xattn_all = _L0_xattn_setup()
    _L0_xattn_in = {k: v for k, v in _L0_xattn_all.items() if k in ('W_q', 'W_kv_down', 'W_kv_up', 'W_out')}
    del _L0_xattn_all

    def _L0_ffn_setup():
        import jax, jax.numpy as jnp
        import numpy as np
        LN_EPS = 1e-05

        def layernorm(x, g, b):
            mu = jnp.mean(x, axis=-1, keepdims=True)
            var = jnp.mean((x - mu) ** 2, axis=-1, keepdims=True)
            return (x - mu) * jax.lax.rsqrt(var + LN_EPS) * g + b

        def act_quant_fake(x):
            scale = 127.0 / jnp.clip(jnp.max(jnp.abs(x), axis=-1, keepdims=True), 1e-05)
            return jnp.clip(jnp.round(x * scale), -128.0, 127.0) / scale

        def weight_quant_fake(w):
            scale = 1.0 / jnp.clip(jnp.mean(jnp.abs(w)), 1e-05)
            return jnp.clip(jnp.round(w * scale), -1.0, 1.0) / scale

        def bitlinear(x, w, b):
            dqx = act_quant_fake(x)
            dqw = weight_quant_fake(w)
            return jnp.einsum('btd,hd->bth', dqx, dqw) + b
        key = jax.random.key(seed)
        ks = jax.random.split(key, 5)
        B, T, D, H = (8, 1024, 256, 1024)
        return {'x': jax.random.normal(ks[0], (B, T, D), dtype=jnp.float32), 'ln1_g': jnp.ones((D,), jnp.float32), 'ln1_b': jnp.zeros((D,), jnp.float32), 'w1': jax.random.normal(ks[1], (H, D), dtype=jnp.float32) * (1.0 / np.sqrt(D)), 'b1': jax.random.normal(ks[2], (H,), dtype=jnp.float32) * 0.02, 'ln2_g': jnp.ones((H,), jnp.float32), 'ln2_b': jnp.zeros((H,), jnp.float32), 'w2': jax.random.normal(ks[3], (D, H), dtype=jnp.float32) * (1.0 / np.sqrt(H)), 'b2': jax.random.normal(ks[4], (D,), jnp.float32) * 0.02}
    _L0_ffn_all = _L0_ffn_setup()
    _L0_ffn_in = {k: v for k, v in _L0_ffn_all.items() if k in ('ln1_g', 'ln1_b', 'w1', 'b1', 'ln2_g', 'ln2_b', 'w2', 'b2')}
    del _L0_ffn_all

    def _L1_attn_setup():
        import jax, jax.numpy as jnp
        import numpy as np
        EMBED_DIM = 256
        NUM_HEADS = 16
        HEAD_DIM = EMBED_DIM // NUM_HEADS
        BATCH = 2
        SEQ = 512
        key = jax.random.key(seed)
        k1, k2, k3, k4, k5 = jax.random.split(key, 5)
        scale_in = 1.0 / np.sqrt(EMBED_DIM)
        return {'x': jax.random.normal(k1, (BATCH, SEQ, EMBED_DIM), dtype=jnp.float32), 'head_mask': jnp.ones((NUM_HEADS,), dtype=jnp.float32), 'qkv_w': jax.random.normal(k2, (3 * EMBED_DIM, EMBED_DIM), dtype=jnp.float32) * scale_in, 'qkv_b': jax.random.normal(k3, (3 * EMBED_DIM,), dtype=jnp.float32) * 0.02, 'fc_w': jax.random.normal(k4, (EMBED_DIM, EMBED_DIM), dtype=jnp.float32) * scale_in, 'fc_b': jax.random.normal(k5, (EMBED_DIM,), dtype=jnp.float32) * 0.02}
    _L1_attn_all = _L1_attn_setup()
    _L1_attn_in = {k: v for k, v in _L1_attn_all.items() if k in ('head_mask', 'qkv_w', 'qkv_b', 'fc_w', 'fc_b')}
    del _L1_attn_all

    def _L1_xattn_setup():
        import jax, jax.numpy as jnp
        import numpy as np
        HEADS = 16
        DIM_HEAD = 64
        SCALE = DIM_HEAD ** (-0.5)

        def _split_heads(x):
            b, l, n = x.shape
            return x.reshape(b, l, HEADS, DIM_HEAD).transpose(0, 2, 1, 3)
        key = jax.random.key(seed)
        ks = jax.random.split(key, 6)
        B, L, D = (4, 512, 256)
        inner = HEADS * DIM_HEAD
        s = lambda fan_in: 1.0 / np.sqrt(fan_in)
        return {'x1': jax.random.normal(ks[0], (B, L, D), jnp.float32), 'x2': jax.random.normal(ks[1], (B, L, D), jnp.float32), 'Wq': jax.random.normal(ks[2], (D, inner), jnp.float32) * s(D), 'Wkv': jax.random.normal(ks[3], (D, 2 * inner), jnp.float32) * s(D), 'Wo': jax.random.normal(ks[4], (inner, D), jnp.float32) * s(inner), 'bo': jax.random.normal(ks[5], (D,), jnp.float32) * 0.02}
    _L1_xattn_all = _L1_xattn_setup()
    _L1_xattn_in = {k: v for k, v in _L1_xattn_all.items() if k in ('Wq', 'Wkv', 'Wo', 'bo')}
    del _L1_xattn_all

    def _L1_ffn_setup():
        import jax, jax.numpy as jnp
        import numpy as np
        TOP_K = 6

        def _glu_mlp(x, wg, wu, wd):
            return jax.nn.silu(x @ wg) * (x @ wu) @ wd
        key = jax.random.key(seed)
        ks = jax.random.split(key, 8)
        B, S, D, E, F, FS = (2, 512, 256, 8, 128, 256)
        sc = 0.02
        return {'hidden_states': jax.random.normal(ks[0], (B, S, D), jnp.float32), 'router_w': jax.random.normal(ks[1], (D, E), jnp.float32) * sc, 'w_gate': jax.random.normal(ks[2], (E, D, F), jnp.float32) * sc, 'w_up': jax.random.normal(ks[3], (E, D, F), jnp.float32) * sc, 'w_down': jax.random.normal(ks[4], (E, F, D), jnp.float32) * sc, 'ws_gate': jax.random.normal(ks[5], (D, FS), jnp.float32) * sc, 'ws_up': jax.random.normal(ks[6], (D, FS), jnp.float32) * sc, 'ws_down': jax.random.normal(ks[7], (FS, D), jnp.float32) * sc}
    _L1_ffn_all = _L1_ffn_setup()
    _L1_ffn_in = {k: v for k, v in _L1_ffn_all.items() if k in ('router_w', 'w_gate', 'w_up', 'w_down', 'ws_gate', 'ws_up', 'ws_down')}
    del _L1_ffn_all
    return {'x': x, 'ctx_1024': ctx_1024, 'itok_BxSx64_0_2047': itok_BxSx64_0_2047, 'L0_attn_W_in': _L0_attn_in['W_in'], 'L0_attn_conv_w': _L0_attn_in['conv_w'], 'L0_attn_conv_b': _L0_attn_in['conv_b'], 'L0_attn_W_xproj': _L0_attn_in['W_xproj'], 'L0_attn_W_dt': _L0_attn_in['W_dt'], 'L0_attn_b_dt': _L0_attn_in['b_dt'], 'L0_attn_A_log': _L0_attn_in['A_log'], 'L0_attn_Dp': _L0_attn_in['Dp'], 'L0_attn_W_out': _L0_attn_in['W_out'], 'L0_xattn_W_q': _L0_xattn_in['W_q'], 'L0_xattn_W_kv_down': _L0_xattn_in['W_kv_down'], 'L0_xattn_W_kv_up': _L0_xattn_in['W_kv_up'], 'L0_xattn_W_out': _L0_xattn_in['W_out'], 'L0_ffn_ln1_g': _L0_ffn_in['ln1_g'], 'L0_ffn_ln1_b': _L0_ffn_in['ln1_b'], 'L0_ffn_w1': _L0_ffn_in['w1'], 'L0_ffn_b1': _L0_ffn_in['b1'], 'L0_ffn_ln2_g': _L0_ffn_in['ln2_g'], 'L0_ffn_ln2_b': _L0_ffn_in['ln2_b'], 'L0_ffn_w2': _L0_ffn_in['w2'], 'L0_ffn_b2': _L0_ffn_in['b2'], 'L1_attn_head_mask': _L1_attn_in['head_mask'], 'L1_attn_qkv_w': _L1_attn_in['qkv_w'], 'L1_attn_qkv_b': _L1_attn_in['qkv_b'], 'L1_attn_fc_w': _L1_attn_in['fc_w'], 'L1_attn_fc_b': _L1_attn_in['fc_b'], 'L1_xattn_Wq': _L1_xattn_in['Wq'], 'L1_xattn_Wkv': _L1_xattn_in['Wkv'], 'L1_xattn_Wo': _L1_xattn_in['Wo'], 'L1_xattn_bo': _L1_xattn_in['bo'], 'L1_ffn_router_w': _L1_ffn_in['router_w'], 'L1_ffn_w_gate': _L1_ffn_in['w_gate'], 'L1_ffn_w_up': _L1_ffn_in['w_up'], 'L1_ffn_w_down': _L1_ffn_in['w_down'], 'L1_ffn_ws_gate': _L1_ffn_in['ws_gate'], 'L1_ffn_ws_up': _L1_ffn_in['ws_up'], 'L1_ffn_ws_down': _L1_ffn_in['ws_down']}

def reference(x, ctx_1024, itok_BxSx64_0_2047, L0_attn_W_in, L0_attn_conv_w, L0_attn_conv_b, L0_attn_W_xproj, L0_attn_W_dt, L0_attn_b_dt, L0_attn_A_log, L0_attn_Dp, L0_attn_W_out, L0_xattn_W_q, L0_xattn_W_kv_down, L0_xattn_W_kv_up, L0_xattn_W_out, L0_ffn_ln1_g, L0_ffn_ln1_b, L0_ffn_w1, L0_ffn_b1, L0_ffn_ln2_g, L0_ffn_ln2_b, L0_ffn_w2, L0_ffn_b2, L1_attn_head_mask, L1_attn_qkv_w, L1_attn_qkv_b, L1_attn_fc_w, L1_attn_fc_b, L1_xattn_Wq, L1_xattn_Wkv, L1_xattn_Wo, L1_xattn_bo, L1_ffn_router_w, L1_ffn_w_gate, L1_ffn_w_up, L1_ffn_w_down, L1_ffn_ws_gate, L1_ffn_ws_up, L1_ffn_ws_down):
    import jax
    import jax.numpy as jnp

    def _L0_attn_ref(x, W_in, conv_w, conv_b, W_xproj, W_dt, b_dt, A_log, Dp, W_out):
        import jax, jax.numpy as jnp
        import numpy as np
        from jax import lax
        B, L, DM = (4, 1024, 256)
        D_INNER, D_STATE, D_CONV, DT_RANK = (512, 16, 4, 64)

        def _silu(v):
            return v * jax.nn.sigmoid(v)

        def _causal_depthwise_conv(xc, conv_w, conv_b):
            k = conv_w[:, None, :]
            y = lax.conv_general_dilated(xc, k, window_strides=(1,), padding=[(D_CONV - 1, 0)], dimension_numbers=('NCH', 'OIH', 'NCH'), feature_group_count=D_INNER)
            return y + conv_b[None, :, None]

        def _mamba_forward(x, W_in, conv_w, conv_b, W_xproj, W_dt, b_dt, A_log, Dp, W_out):
            xz = jnp.einsum('bld,de->ble', x, W_in)
            xin, z = jnp.split(xz, 2, axis=-1)
            xc = _causal_depthwise_conv(xin.transpose(0, 2, 1), conv_w, conv_b)
            xc = _silu(xc).transpose(0, 2, 1)
            x_dbl = jnp.einsum('bld,de->ble', xc, W_xproj)
            dt, Bm, Cm = jnp.split(x_dbl, [DT_RANK, DT_RANK + D_STATE], axis=-1)
            dt = jax.nn.softplus(jnp.einsum('blr,rd->bld', dt, W_dt) + b_dt)
            A = -jnp.exp(A_log)

            def step(h, inp):
                dt_t, B_t, C_t, x_t = inp
                dA = jnp.exp(dt_t[..., None] * A)
                dBx = dt_t[..., None] * B_t[:, None, :] * x_t[..., None]
                h = dA * h + dBx
                y_t = jnp.sum(h * C_t[:, None, :], axis=-1)
                return (h, y_t)
            h0 = jnp.zeros((x.shape[0], D_INNER, D_STATE), x.dtype)
            xs = (dt.transpose(1, 0, 2), Bm.transpose(1, 0, 2), Cm.transpose(1, 0, 2), xc.transpose(1, 0, 2))
            _, ys = lax.scan(step, h0, xs)
            y = ys.transpose(1, 0, 2) + xc * Dp
            y = y * _silu(z)
            return jnp.einsum('bld,de->ble', y, W_out)
        return _mamba_forward(x, W_in, conv_w, conv_b, W_xproj, W_dt, b_dt, A_log, Dp, W_out)

    def _L0_xattn_ref(x_q, x_kv, indices, W_q, W_kv_down, W_kv_up, W_out):
        import jax, jax.numpy as jnp
        import numpy as np
        B, NQ, NKV, K = (2, 256, 512, 64)
        D, H, LAT = (256, 16, 128)
        HD = D // H
        SCALE = 1.0 / np.sqrt(HD)
        b, nq, d = x_q.shape
        q = (x_q @ W_q.T).reshape(b, nq, H, HD)
        c_kv = x_kv @ W_kv_down.T
        c_sel = c_kv[jnp.arange(b)[:, None, None], indices]
        kv = (c_sel @ W_kv_up.T).reshape(b, nq, K, 2, H, HD)
        k = kv[:, :, :, 0]
        v = kv[:, :, :, 1]
        scores = jnp.einsum('bqhd,bqkhd->bqkh', q, k) * SCALE
        attn = jax.nn.softmax(scores, axis=2)
        out = jnp.einsum('bqkh,bqkhd->bqhd', attn, v).reshape(b, nq, d)
        return out @ W_out.T

    def _L0_ffn_ref(x, ln1_g, ln1_b, w1, b1, ln2_g, ln2_b, w2, b2):
        import jax, jax.numpy as jnp
        import numpy as np
        LN_EPS = 1e-05

        def layernorm(x, g, b):
            mu = jnp.mean(x, axis=-1, keepdims=True)
            var = jnp.mean((x - mu) ** 2, axis=-1, keepdims=True)
            return (x - mu) * jax.lax.rsqrt(var + LN_EPS) * g + b

        def act_quant_fake(x):
            scale = 127.0 / jnp.clip(jnp.max(jnp.abs(x), axis=-1, keepdims=True), 1e-05)
            return jnp.clip(jnp.round(x * scale), -128.0, 127.0) / scale

        def weight_quant_fake(w):
            scale = 1.0 / jnp.clip(jnp.mean(jnp.abs(w)), 1e-05)
            return jnp.clip(jnp.round(w * scale), -1.0, 1.0) / scale

        def bitlinear(x, w, b):
            dqx = act_quant_fake(x)
            dqw = weight_quant_fake(w)
            return jnp.einsum('btd,hd->bth', dqx, dqw) + b
        h = layernorm(x, ln1_g, ln1_b)
        h = bitlinear(h, w1, b1)
        h = jax.nn.gelu(h, approximate=False)
        h = layernorm(h, ln2_g, ln2_b)
        h = bitlinear(h, w2, b2)
        return h

    def _L1_attn_ref(x, head_mask, qkv_w, qkv_b, fc_w, fc_b):
        import jax, jax.numpy as jnp
        import numpy as np
        EMBED_DIM = 256
        NUM_HEADS = 16
        HEAD_DIM = EMBED_DIM // NUM_HEADS
        BATCH = 2
        SEQ = 512
        N, S, D = x.shape
        H, hd = (NUM_HEADS, HEAD_DIM)
        qkv = jnp.einsum('nsd,ed->nse', x, qkv_w) + qkv_b
        qkv = qkv.reshape(N, S, H, 3, hd).transpose(3, 0, 2, 1, 4)
        q, k, v = (qkv[0], qkv[1], qkv[2])
        hm = head_mask.reshape(1, H, 1, 1)
        q = q * hm
        k = k * hm
        v = v * hm
        energy = jnp.einsum('nhqd,nhkd->nhqk', q, k)
        attention = jax.nn.softmax(energy / jnp.sqrt(jnp.float32(hd)), axis=-1)
        out = jnp.einsum('nhqk,nhkd->nhqd', attention, v)
        out = out.transpose(0, 2, 1, 3).reshape(N, S, H * hd)
        out = jnp.einsum('nsd,ed->nse', out, fc_w) + fc_b
        return out

    def _L1_xattn_ref(x1, x2, Wq, Wkv, Wo, bo):
        import jax, jax.numpy as jnp
        import numpy as np
        HEADS = 16
        DIM_HEAD = 64
        SCALE = DIM_HEAD ** (-0.5)

        def _split_heads(x):
            b, l, n = x.shape
            return x.reshape(b, l, HEADS, DIM_HEAD).transpose(0, 2, 1, 3)
        q = x1 @ Wq
        kv = x2 @ Wkv
        k, v = jnp.split(kv, 2, axis=-1)
        q, k, v = map(_split_heads, (q, k, v))
        attn = jnp.einsum('bhid,bhjd->bhij', q, k) * SCALE
        attn = jax.nn.softmax(attn, axis=-1)
        out = jnp.einsum('bhij,bhjd->bhid', attn, v)
        b, h, l, d = out.shape
        out = out.transpose(0, 2, 1, 3).reshape(b, l, h * d)
        return out @ Wo + bo

    def _L1_ffn_ref(hidden_states, router_w, w_gate, w_up, w_down, ws_gate, ws_up, ws_down):
        import jax, jax.numpy as jnp
        import numpy as np
        TOP_K = 6

        def _glu_mlp(x, wg, wu, wd):
            return jax.nn.silu(x @ wg) * (x @ wu) @ wd
        B, S, D = hidden_states.shape
        x = hidden_states.reshape(-1, D)
        scores = jax.nn.softmax(x @ router_w, axis=-1)
        topk_w, topk_idx = jax.lax.top_k(scores, TOP_K)
        g = jnp.einsum('td,edf->etf', x, w_gate)
        u = jnp.einsum('td,edf->etf', x, w_up)
        f_all = jnp.einsum('etf,efd->ted', jax.nn.silu(g) * u, w_down)
        picked = jnp.take_along_axis(f_all, topk_idx[:, :, None], axis=1)
        y = jnp.sum(picked * topk_w[:, :, None], axis=1).reshape(B, S, D)
        y = y + _glu_mlp(hidden_states, ws_gate, ws_up, ws_down)
        return y
    x = _layernorm(x + _L0_attn_ref(x, L0_attn_W_in, L0_attn_conv_w, L0_attn_conv_b, L0_attn_W_xproj, L0_attn_W_dt, L0_attn_b_dt, L0_attn_A_log, L0_attn_Dp, L0_attn_W_out), axis=-1)
    x = _layernorm(x + _L0_xattn_ref(x, ctx_1024, itok_BxSx64_0_2047, L0_xattn_W_q, L0_xattn_W_kv_down, L0_xattn_W_kv_up, L0_xattn_W_out), axis=-1)
    x = _layernorm(x + _L0_ffn_ref(x, L0_ffn_ln1_g, L0_ffn_ln1_b, L0_ffn_w1, L0_ffn_b1, L0_ffn_ln2_g, L0_ffn_ln2_b, L0_ffn_w2, L0_ffn_b2), axis=-1)
    x = _layernorm(x + _L1_attn_ref(x, L1_attn_head_mask, L1_attn_qkv_w, L1_attn_qkv_b, L1_attn_fc_w, L1_attn_fc_b), axis=-1)
    x = _layernorm(x + _L1_xattn_ref(x, ctx_1024, L1_xattn_Wq, L1_xattn_Wkv, L1_xattn_Wo, L1_xattn_bo), axis=-1)
    x = _layernorm(x + _L1_ffn_ref(x, L1_ffn_router_w, L1_ffn_w_gate, L1_ffn_w_up, L1_ffn_w_down, L1_ffn_ws_gate, L1_ffn_ws_up, L1_ffn_ws_down), axis=-1)
    return x

_drawn_inputs = setup_inputs


def setup_inputs(seed=0):
    import zlib

    import numpy as np

    out = dict(_drawn_inputs(seed))
    spreads = {'L0_attn_conv_b': (0.0, 0.8),
     'L0_attn_b_dt': (-4.599999904632568, 0.6),
     'L0_attn_Dp': (1.0, 0.6),
     'L0_ffn_ln1_g': (1.0, 0.2),
     'L0_ffn_ln1_b': (0.0, 0.1),
     'L0_ffn_ln2_g': (1.0, 0.2),
     'L0_ffn_ln2_b': (0.0, 0.1)}
    factors = {'L0_attn_W_in': 7.387,
     'L0_attn_conv_w': 8.0,
     'L0_attn_W_xproj': 8.0,
     'L0_attn_W_dt': 8.0,
     'L0_attn_A_log': 8.0,
     'L0_attn_W_out': 7.421,
     'L0_ffn_b1': 2.685,
     'L0_ffn_b2': 3.12,
     'L1_attn_qkv_b': 3.052,
     'L1_attn_fc_b': 3.572,
     'L1_xattn_bo': 3.075,
     'L1_ffn_router_w': 8.0,
     'L1_ffn_w_gate': 8.0,
     'L1_ffn_w_up': 8.0,
     'L1_ffn_w_down': 8.0,
     'L1_ffn_ws_gate': 3.198,
     'L1_ffn_ws_up': 3.243,
     'L1_ffn_ws_down': 3.158}
    for name, (base, spread) in spreads.items():
        noise = np.random.default_rng([zlib.crc32(name.encode()), seed]).standard_normal(out[name].shape)
        drawn = base * np.exp(spread * noise) if base else spread * noise
        out[name] = jnp.asarray(drawn.astype(out[name].dtype))
    for name, factor in factors.items():
        out[name] = (out[name] * factor).astype(out[name].dtype)
    return out
```

```python
from contextlib import ExitStack

import numpy as np

import concourse.bass as bass
from concourse import mybir

F32 = mybir.dt.float32
BF16 = mybir.dt.bfloat16
I32 = mybir.dt.int32
ALU = mybir.AluOpType
ACT = mybir.ActivationFunctionType
AX = mybir.AxisListType.X

P = 128
B, T, D = 16, 256, 256
TT = T // P
KD = D // P
DI, NS, TAPS, RANK = 512, 16, 4, 64
M = DI // P
NG = 4
STEPS = NS // NG
SEL = 64
H = 16
FF = 1024
KF = FF // P
E, TOPK, FE = 8, 6, 128
MOE = E * FE + 256
KM = MOE // P
EPS = 1e-5
ROUND = 12582912.0
MASKED = -1e30
HUGE = 3e38
EXP_LN = "natural_log_exp_and_others"
SILU_SET = "silu_and_others"
GELU_SET = "gelu_and_others"


def at(i, per, n):
    return i * per + n


class Chain:

    def __init__(self, eng, sem, i, per):
        self.eng, self.sem, self.i, self.per, self.n = eng, sem, i, per, 0

    def did(self, ins):
        self.n += 1
        return ins.then_inc(self.sem, 1)

    def settle(self):
        self.eng.wait_ge(self.sem, at(self.i, self.per, self.n))

    def link(self, ins):
        self.did(ins)
        self.settle()

    def close(self):
        assert self.n == self.per, f"steps per sequence: {self.n}, stated {self.per}"


V_STEPS = 112
A_STEPS = 10

CONST_INPUTS = [
    ("win", (P, KD, 2 * DI), F32), ("wxd", (P, M, RANK), F32), ("wbc", (P, M, 96), F32),
    ("wdt", (RANK, DI), F32), ("wout", (P, M, D), F32),
    ("convw", (P, M, TAPS), F32), ("convb", (P, M), F32), ("bdt", (P, M), F32),
    ("alog", (P, M, NS), F32), ("dp", (P, M), F32),
    ("ident", (P, P), F32), ("identb", (P, P), BF16), ("sel", (96, 32), BF16),
    ("iota", (P, 32), BF16), ("group", (P, 2), F32), ("half", (P, 1), F32), ("ones", (P, P), F32), ("tri", (P, E, E), F32),
    ("wq0", (P, KD, 512), F32), ("wdown0", (P, KD, P), F32), ("wk0", (P, 512), F32),
    ("wv0", (P, D), F32), ("wo0", (P, 4, D), F32),
    ("ln1g", (P, D), F32), ("ln1b", (P, D), F32), ("fb2", (P, D), F32),
    ("wq1", (P, KD, 512), F32), ("wk1", (P, KD, 512), F32), ("wv1", (P, KD, D), F32),
    ("qb1", (P, 4), F32), ("kb1", (P, 4), F32), ("hm1", (P, 4), F32),
    ("vb1", (P, D), F32), ("hmv1", (P, D), F32), ("wo1", (P, 4, D), F32), ("ob1", (P, D), F32),
    ("wq2", (P, KD, 1024), F32), ("wk2", (P, KD, 1024), F32), ("wv2", (P, KD, 1024), F32),
    ("wo2", (P, 8, D), F32), ("ob2", (P, D), F32),
    ("router", (P, KD, E), F32), ("wgate", (P, KD, MOE), F32), ("wup", (P, KD, MOE), F32),
    ("wmoe", (P, KM, D), F32),
]


def build(nc, dram, out):
    ctx = ExitStack()
    with ctx:
        def sb(name, shape, dt=F32):
            return ctx.enter_context(nc.sbuf_tensor(name, list(shape), dt))

        def sem(name):
            return ctx.enter_context(nc.semaphore(name))

        W = {name: sb(name, shape, dt) for name, shape, dt in CONST_INPUTS}
        aneg = sb("aneg", (P, M, NS))
        w1q = sb("w1q", (P, KD, FF), BF16)
        w2q = sb("w2q", (P, KF, D), BF16)
        wscale = sb("wscale", (P, 8))
        epsc = sb("epsc", (P, 1))
        onec = sb("onec", (P, 1))

        x_in = sb("x_in", (P, TT, D))
        xT_in = sb("xT_in", (P, KD, T))
        ctxT = sb("ctxT", (P, KD, T))
        idx = sb("idx", (P, P), I32)
        x = sb("x", (P, TT, D))
        xT = sb("xT", (P, KD, T))
        res_out = sb("res_out", (P, 2, TT, D))
        res, x_out = res_out[:, 0], res_out[:, 1]
        mask = sb("mask", (P, TT, T))
        stats = sb("stats", (P, TT, 2, 6))
        mv = sb("mv", (P, TT, 2))
        lnv = sb("lnv", (P, TT))
        rstd = sb("rstd", (P, TT))
        nt = sb("nt", (P, TT))
        small = sb("small", (P, 8, TT))
        smask1 = sb("smask1", (P, 2, T))
        spare = sb("spare", (P, 9 + TT * H // 2))
        rmax = sb("rmax", (P, TT * H))
        rsum = sb("rsum", (P, TT * H))
        rinv = sb("rinv", (P, TT * H))
        route = sb("route", (P, 6, TT, E))
        rs2 = sb("rs2", (P, 4, TT))
        kbh = sb("kbh", (P, 2, 4))
        hmk = sb("hmk", (P, 2, 4))
        hmq = sb("hmq", (P, 4))

        ARENA = 15120
        arena = sb("arena", (P, ARENA))

        def carve(start, shape, dt=F32):
            n = int(np.prod(shape))
            words = n if dt != BF16 else n // 2
            assert start + words <= ARENA, (start, shape)
            ap = arena[:, start:start + words]
            if dt != F32:
                ap = ap.bitcast(dt)
            if len(shape) > 1:
                names = "abcd"[:len(shape)]
                sizes = {c: s for c, s in zip(names, shape)}
                ap = ap.rearrange(f"p ({' '.join(names)}) -> p {' '.join(names)}", **sizes)
            return ap

        PAD = T + TAPS - 1
        xin = carve(0, (M, PAD))
        dtx = carve(0, (M, T))
        conv = carve(1036, (M, T))
        yT = carve(1036, (M, T))
        xc = carve(2060, (M, T))
        zs = carve(3084, (M, T))
        dt = carve(4108, (M, T))
        csb = carve(5132, (NS, T))
        decay = [carve(9228 + 1024 * s, (NG, T)) for s in range(2)]
        hbuf = [carve(11276 + 1024 * s, (NG, T)) for s in range(2)]
        hc = [carve(13324, (NG, T)),
              res_out[:].rearrange("p a t d -> p (a t) d")]
        dtr = carve(14348, (T,))
        bcs = carve(14604, (T,), BF16)
        bmid = carve(14732, (T,), BF16)
        br1 = carve(14860, (T,))
        sp_x = carve(5132, (M, T))
        sp_e = carve(6156, (M, T))
        sp_l = carve(7180, (M, T))
        oh_hi = carve(9228, (P, 32), BF16)
        oh_lo = carve(11276, (P, 16), BF16)
        cnt = carve(12300, (P, 16), BF16)
        cm1 = carve(13324, (TT, T))
        cm0 = carve(13836, (TT, T))
        ix = [carve(8204 + 128 * s, (P,)) for s in range(6)]
        ixi = [a.bitcast(I32) for a in ix]
        hib = carve(8204 + 768, (P,), BF16)
        lob = carve(8204 + 832, (P,), BF16)

        QT = carve(0, (8, T))
        KT = carve(2048, (8, T))
        VV = carve(4096, (TT, 1024))
        VP = VV.rearrange("p t (h d) -> p t h d", h=2 * H)[:, :, 0:H, :]
        OT = carve(6144, (8, T))
        ln2g, ln2b, fb1 = carve(8192, (FF,)), carve(9216, (FF,)), carve(13568, (FF,))
        prob = [carve(10240 + 512 * s, (2, T)) for s in range(3)]
        probT = [carve(11776 + 512 * s, (4, P)) for s in range(2)]
        smask = [carve(12800, (2, T)), smask1[:, :, :]]
        ckvT = carve(13312, (T,))
        ckvT2 = carve(8192, (TT, D))

        fh = carve(0, (TT, FF))
        fq = carve(2048, (TT, FF))
        qb = carve(4096, (TT, FF), BF16)
        qT = carve(5120, (KF, T), BF16)
        wst = carve(6144, (KD, FF))
        wst2 = carve(8192, (KD, FF))

        sg = carve(0, (TT, MOE))
        mh = carve(2560, (TT, MOE))
        mhT = carve(5120, (KM, T))
        rcmp = carve(7680, (2, TT, E, E))

        ps = ctx.enter_context(nc.psum_tensor("ps", [P, 8, 512], F32))

        def bank(n, a=None):
            ap = ps[:, n, :]
            return ap.rearrange("p (a b) -> p a b", a=a or 2)

        w_first, w_rest, staged = sem("w_first"), sem("w_rest"), sem("staged")
        setup_v, setup_a, setup_t = sem("setup_v"), sem("setup_a"), sem("setup_t")
        batch_done, rows_loaded = sem("batch_done"), sem("rows_loaded")
        loaded, ctx_loaded, stored = sem("loaded"), sem("ctx_loaded"), sem("stored")
        v_step, a_step = sem("v_step"), sem("a_step")
        xz = sem("xz")
        xin_sb = sem("xin_sb")
        conv_done = sem("conv_done")
        silu_x, silu_z = sem("silu_x"), sem("silu_z")
        onehot = sem("onehot")
        idx_read, pads = sem("idx_read"), sem("pads")
        cnt_ps, cnt_sb, cntT, cnt_max, cnt_ln = sem("cnt_ps"), sem("cnt_sb"), sem("cntT"), sem("cnt_max"), sem("cnt_ln")
        xdbl, dtr_sb, bc_split = sem("xdbl"), sem("dtr_sb"), sem("bc_split")
        dt_ps, dt_x, dt_ln, dt_done = sem("dt_ps"), sem("dt_x"), sem("dt_ln"), sem("dt_done")
        c_ps, c_sb = sem("c_ps"), sem("c_sb")
        b_ps, b_used, decay_ready, h_ready, hc_ready, y_ready, y_done = (
            sem("b_ps"), sem("b_used"), sem("decay_ready"), sem("h_ready"), sem("hc_ready"),
            sem("y_ready"), sem("y_done"))
        sum_ps, sum_read = sem("sum_ps"), sem("sum_read")
        x_ready, xT_ps, xT_ready = sem("x_ready"), sem("xT_ps"), sem("xT_ready")
        var_ready, rstd_guess = sem("var_ready"), sem("rstd_guess")
        f_q, f_qT_ps, f_qT, f_h_ps, f_h, f_gelu = (
            sem("f_q"), sem("f_qT_ps"), sem("f_qT"), sem("f_h_ps"), sem("f_h"), sem("f_gelu"))
        r_ps, r_max, r_exp, r_w = sem("r_ps"), sem("r_max"), sem("r_exp"), sem("r_w")
        gu_ps, gu_silu, moe_h, moe_hT_ps, moe_hT = (
            sem("gu_ps"), sem("gu_silu"), sem("moe_h"), sem("moe_hT_ps"), sem("moe_hT"))

        FIRST = [n for n, (name, _, _) in enumerate(CONST_INPUTS) if n <= 17 or name in ("kb1", "hm1")]
        REST = [n for n in range(len(CONST_INPUTS)) if n not in FIRST]

        class Attention:

            UNITS = TT * H // 2

            def __init__(self, tag, hd, masked):
                self.hd, self.masked = hd, masked
                self.tiles = 4 if hd == 16 else 8
                self.proj = sem(tag + "_proj")
                self.evac = sem(tag + "_evac")
                self.vevac = sem(tag + "_vevac")
                self.s_ps = sem(tag + "_s_ps")
                self.rmax = sem(tag + "_rmax")
                self.probs = sem(tag + "_probs")
                self.pT_ps = sem(tag + "_pT_ps")
                self.pT = sem(tag + "_pT")
                self.pv = sem(tag + "_pv")
                self.inv = sem(tag + "_inv")
                self.norm = sem(tag + "_norm")
                self.o = sem(tag + "_o")

            def rows(self, h):
                if self.hd == 16:
                    group = h // 4
                    return slice(64 * (group // 2), 64 * (group // 2) + 64), h % 4, 4 * (group % 2) + h % 4
                return slice(64 * (h // 8), 64 * (h // 8) + 64), h % 8, h % 8

            def heads(self, u):
                return [2 * (u % (H // 2)), 2 * (u % (H // 2)) + 1], u // (H // 2)

            def out_rows(self, u, j):
                if self.hd == 16:
                    start = 64 * (u % 2) + 32 * j
                    return slice(start, start + 32)
                return slice(64 * j, 64 * j + 64)

            def out_tile(self, u):
                hp = u % (H // 2)
                return hp // 2 if self.hd == 16 else hp

            def unit_rows(self, u):
                return slice(64 * (u % 2), 64 * (u % 2) + 64) if self.hd == 16 else slice(0, P)

        att0 = Attention("lat", 16, True)
        att1 = Attention("self", 16, False)
        att2 = Attention("cross", 64, False)

        block = ctx.enter_context(nc.Block())

        @block.sync
        def _(sp):
            sp.sem_inc(stored, 16)
            for n in FIRST:
                name, shape, _ = CONST_INPUTS[n]
                sp.dma_start(W[name][:], dram[name]).then_inc(w_first, 16)

            def load(i):
                sp.dma_start(x_in[:], dram["x"][i].rearrange("a p d -> p a d")).then_inc(loaded, 16)
                sp.dma_start(xT_in[:], dram["xT"][i].rearrange("a p d -> p a d")).then_inc(loaded, 16)
                sp.dma_start(idx[:], dram["idx"][i]).then_inc(loaded, 16)

            def load_ctx(i):
                sp.dma_start(ctxT[:], dram["ctxT"][i].rearrange("a p d -> p a d")).then_inc(ctx_loaded, 16)

            def load_rows():
                for row, name in ((fb1, "fb1"), (ln2g, "ln2g"), (ln2b, "ln2b")):
                    sp.dma_start(row, dram[name]).then_inc(rows_loaded, 16)

            def store(i):
                sp.dma_start(out[i].rearrange("a p d -> p a d"), x_out).then_inc(stored, 16)

            load(0)
            sp.dma_start(wst, dram["w1"]).then_inc(staged, 16)
            sp.dma_start(wst2, dram["w2"].rearrange("p a b -> p (a b)")).then_inc(staged, 16)
            load_ctx(0)
            for n in REST:
                name, shape, _ = CONST_INPUTS[n]
                sp.dma_start(W[name][:], dram[name]).then_inc(w_rest, 16)
            with sp.Fori(0, B - 1) as i:
                sp.wait_ge(sum_read, at(i, 6, 1))
                load_rows()
                load(i + 1)
                sp.wait_ge(att2.evac, at(i, 4, 4))
                sp.wait_ge(att2.vevac, at(i, 8, 8))
                load_ctx(i + 1)
                sp.wait_ge(batch_done, i + 2)
                store(i)
            sp.wait_ge(sum_read, at(B - 1, 6, 1))
            load_rows()
            sp.wait_ge(batch_done, B + 1)
            store(B - 1)
            sp.wait_ge(stored, 16 * (B + 1))

        @block.tensor
        def _(pe):
            mm, tr = nc.tensor.matmul, nc.tensor.transpose

            pe.wait_ge(setup_v, 2)
            pe.wait_ge(w_first, 16 * len(FIRST))
            mm(ps[:, 0, 0:2], W["ones"][:], wscale[:, 0:2], start=True, stop=True).then_inc(setup_t, 1)

            def x_transposed(i, version, nth):
                pe.wait_ge(x_ready, at(i, 5, version))
                for tt in range(TT):
                    for k in range(KD):
                        last = tr(ps[:, 7, k * T + tt * P:k * T + (tt + 1) * P],
                                  x[:, tt, k * P:(k + 1) * P], W["ident"][:])
                last.then_inc(xT_ps, 1)
                pe.wait_ge(xT_ready, at(i, 4, nth))

            def mamba(i):
                pe.wait_ge(batch_done, i + 1)
                pe.wait_ge(loaded, at(i, 48, 48))
                for m in range(2 * M):
                    for k in range(KD):
                        last = mm(bank(m // 2)[:, m % 2, :], W["win"][:, k, m * P:(m + 1) * P],
                                  xT_in[:, k, :], start=(k == 0), stop=(k == KD - 1))
                    if m % 2:
                        last.then_inc(xz, 1)
                pe.wait_ge(onehot, at(i, 2, 2))
                for q in range(P):
                    last = mm(ps[0:32, 4 + q // 32, (q % 32) * 16:(q % 32) * 16 + 16],
                              oh_hi[:, q, :], oh_lo[:, q, :], start=True, stop=True)
                    if q % 32 == 31:
                        last.then_inc(cnt_ps, 1)
                pe.wait_ge(cnt_sb, at(i, 4, 4))
                for k in range(M):
                    pe.wait_ge(silu_x, at(i, M, k + 1))
                    mm(ps[0:RANK, 4, 0:T], W["wxd"][:, k, :], xc[:, k, :], start=(k == 0), stop=(k == M - 1))
                    last = mm(ps[0:96, 5, 0:T], W["wbc"][:, k, :], xc[:, k, :], start=(k == 0), stop=(k == M - 1))
                last.then_inc(xdbl, 1)
                psb = ps[:, 6, :].bitcast(BF16)
                for lo in range(16):
                    last = tr(psb[:, lo * 32:lo * 32 + 32], cnt[0:32, :, lo], W["identb"][0:32, 0:32])
                last.then_inc(cntT, 1)
                pe.wait_ge(dtr_sb, at(i, 1, 1))
                pe.wait_ge(cnt_max, at(i, 1, 1))
                for m in range(M):
                    last = mm(bank(6 + m // 2)[:, m % 2, :], W["wdt"][:, m * P:(m + 1) * P],
                              dtr[0:RANK, :], start=True, stop=True)
                    if m % 2:
                        last.then_inc(dt_ps, 1)
                pe.wait_ge(bc_split, at(i, 1, 1))
                pe.wait_ge(silu_z, at(i, 1, 1))
                for n in range(NS):
                    if n % 2 == 0 and n >= 8:
                        pe.wait_ge(c_sb, at(i, 8, n // 2 - 3))
                    last = mm(bank(n // 2 % 4)[:, n % 2, :], W["sel"][:, 16 + n:17 + n].to_broadcast([96, P]),
                              bcs[0:96, :], start=True, stop=True)
                    if n % 2:
                        last.then_inc(c_ps, 1)
                pe.wait_ge(c_sb, at(i, 8, 8))

                def spread_b(u):
                    if u >= 2:
                        pe.wait_ge(b_used, at(i, M * STEPS, u - 1))
                    for n in range(NG):
                        s = u % STEPS * NG + n
                        last = mm(bank(u % 2 * 2 + n // 2)[:, n % 2, :],
                                  W["sel"][:, s:s + 1].to_broadcast([96, P]), bcs[0:96, :],
                                  start=True, stop=True)
                    last.then_inc(b_ps, 1)

                def sum_states(u):
                    m, g = u // STEPS, u % STEPS
                    pe.wait_ge(hc_ready, at(i, M * STEPS, u + 1))
                    if g == 0 and m >= 2:
                        pe.wait_ge(y_done, at(i, M, m - 1))
                    for n in range(NG):
                        last = mm(ps[:, 4 + m % 2, 0:T], W["ident"][:], hc[u % 2][:, n, :],
                                  start=(g == 0 and n == 0), stop=(g == STEPS - 1 and n == NG - 1))
                    last.then_inc(y_ready, 1)

                spread_b(0)
                spread_b(1)
                for u in range(M * STEPS):
                    if u + 2 < M * STEPS:
                        spread_b(u + 2)
                    sum_states(u)
                pe.wait_ge(y_done, at(i, M, M))
                for tt in range(TT):
                    for m in range(M):
                        last = mm(bank(6)[:, tt, :], yT[:, m, tt * P:(tt + 1) * P], W["wout"][:, m, :],
                                  start=(m == 0), stop=(m == M - 1))
                last.then_inc(sum_ps, 1)

            def attention(i, a, wo):
                hd = a.hd

                def scores(u):
                    hs, qt = a.heads(u)
                    if u >= 3:
                        pe.wait_ge(a.probs, at(i, a.UNITS, u - 2))
                    for j, h in enumerate(hs):
                        r, tq, tk = a.rows(h)
                        last = mm(bank(u % 3)[:, j, :], QT[r, tq, qt * P:(qt + 1) * P], KT[r, tk, :],
                                  start=True, stop=True)
                    last.then_inc(a.s_ps, 1)

                def turn(u):
                    pe.wait_ge(a.norm, at(i, a.UNITS, u + 1))
                    if u >= 2:
                        pe.wait_ge(a.pT, at(i, a.UNITS, u - 1))
                    for j in range(2):
                        for jt in range(TT):
                            last = tr(bank(3 + u % 2, 4)[:, 2 * j + jt, :],
                                      prob[u % 3][:, j, jt * P:(jt + 1) * P], W["ident"][:])
                    last.then_inc(a.pT_ps, 1)

                def times_v(u):
                    hs, qt = a.heads(u)
                    pe.wait_ge(a.pT, at(i, a.UNITS, u + 1))
                    if u >= 2:
                        pe.wait_ge(a.o, at(i, a.UNITS, u - 1))
                    for j, h in enumerate(hs):
                        for jt in range(TT):
                            w = VP[:, jt, h, :] if hd == 16 else VV[:, jt, h * hd:(h + 1) * hd]
                            last = mm(ps[a.out_rows(u, j), 5 + u % 2, 0:P], w, probT[u % 2][:, 2 * j + jt, :],
                                      start=(jt == 0), stop=(jt == TT - 1))
                    last.then_inc(a.pv, 1)

                for u in range(a.UNITS + 4):
                    if u < a.UNITS:
                        scores(u)
                    if 0 <= u - 2 < a.UNITS:
                        turn(u - 2)
                    if 0 <= u - 4:
                        times_v(u - 4)
                for tt in range(TT):
                    pe.wait_ge(a.o, at(i, a.UNITS, (tt + 1) * (H // 2)))
                    for k in range(a.tiles):
                        last = mm(bank(7)[:, tt, :], OT[:, k, tt * P:(tt + 1) * P], wo[:, k, :],
                                  start=(k == 0), stop=(k == a.tiles - 1))
                last.then_inc(sum_ps, 1)

            def latent_projections(i):
                pe.wait_ge(w_rest, 16 * len(REST))
                pe.wait_ge(ctx_loaded, at(i, 16, 16))
                for k in range(KD):
                    last = mm(ps[:, 5, 0:T], W["wdown0"][:, k, :], ctxT[:, k, :], start=(k == 0), stop=(k == KD - 1))
                last.then_inc(att0.proj, 1)
                for t in range(4):
                    for k in range(KD):
                        last = mm(bank(t // 2)[:, t % 2, :], W["wq0"][:, k, t * P:(t + 1) * P], xT[:, k, :],
                                  start=(k == 0), stop=(k == KD - 1))
                last.then_inc(att0.proj, 1)
                pe.wait_ge(att0.evac, at(i, 3, 1))
                for t in range(4):
                    last = mm(bank(2 + t // 2)[:, t % 2, :], W["wk0"][:, t * P:(t + 1) * P], ckvT,
                              start=True, stop=True)
                last.then_inc(att0.proj, 1)
                for tt in range(TT):
                    last = mm(bank(4)[:, tt, :], ckvT[:, tt * P:(tt + 1) * P], W["wv0"][:], start=True, stop=True)
                last.then_inc(att0.proj, 1)
                pe.wait_ge(att0.evac, at(i, 3, 3))
                pe.wait_ge(att0.vevac, at(i, 1, 1))

            def self_projections(i):
                for first, w in ((0, W["wq1"]), (2, W["wk1"])):
                    for t in range(4):
                        for k in range(KD):
                            last = mm(bank(first + t // 2)[:, t % 2, :], w[:, k, t * P:(t + 1) * P], xT[:, k, :],
                                      start=(k == 0), stop=(k == KD - 1))
                    last.then_inc(att1.proj, 1)
                for tt in range(TT):
                    for k in range(KD):
                        last = mm(bank(4)[:, tt, :], xT[:, k, tt * P:(tt + 1) * P], W["wv1"][:, k, :],
                                  start=(k == 0), stop=(k == KD - 1))
                last.then_inc(att1.proj, 1)
                pe.wait_ge(att1.evac, at(i, 1, 1))
                pe.wait_ge(att1.vevac, at(i, 2, 2))

            def cross_projections(i):
                for n, b in enumerate((0, 1, 2, 7)):
                    for t in (2 * n, 2 * n + 1):
                        for k in range(KD):
                            last = mm(bank(b)[:, t % 2, :], W["wq2"][:, k, t * P:(t + 1) * P], xT[:, k, :],
                                      start=(k == 0), stop=(k == KD - 1))
                    last.then_inc(att2.proj, 1)
                for n in range(4):
                    for t in (2 * n, 2 * n + 1):
                        for k in range(KD):
                            last = mm(bank(3 + n)[:, t % 2, :], W["wk2"][:, k, t * P:(t + 1) * P], ctxT[:, k, :],
                                      start=(k == 0), stop=(k == KD - 1))
                    last.then_inc(att2.proj, 1)
                for n in range(4):
                    b = (0, 1, 2, 7)[n]
                    pe.wait_ge(att2.vevac, at(i, 8, n + 1))
                    for k in range(KD):
                        last = mm(ps[:, b, :], ctxT[:, k, n // 2 * P:(n // 2 + 1) * P],
                                  W["wv2"][:, k, n % 2 * 512:(n % 2 + 1) * 512],
                                  start=(k == 0), stop=(k == KD - 1))
                    last.then_inc(att2.proj, 1)
                pe.wait_ge(att2.evac, at(i, 4, 4))
                pe.wait_ge(att2.vevac, at(i, 8, 8))

            def ffn(i):
                psb = ps[:, 6, :].bitcast(BF16).rearrange("p (a b) -> p a b", b=T)
                pe.wait_ge(f_q, at(i, 2, 1))
                for tt in range(TT):
                    for k in range(KD):
                        last = tr(psb[:, k, tt * P:(tt + 1) * P], qb[:, tt, k * P:(k + 1) * P], W["identb"][:])
                last.then_inc(f_qT_ps, 1)
                pe.wait_ge(f_qT, at(i, 3, 1))
                for tt in range(TT):
                    for half in range(2):
                        for k in range(KD):
                            last = mm(ps[:, 2 * tt + half, :], qT[:, k, tt * P:(tt + 1) * P],
                                      w1q[:, k, half * 512:(half + 1) * 512], start=(k == 0), stop=(k == KD - 1))
                    last.then_inc(f_h_ps, 1)
                pe.wait_ge(f_q, at(i, 2, 2))
                for n in range(2):
                    psb = ps[:, 4 + n, :].bitcast(BF16).rearrange("p (a b) -> p a b", b=T)
                    for k in range(4):
                        for tt in range(TT):
                            last = tr(psb[:, k, tt * P:(tt + 1) * P],
                                      qb[:, tt, (4 * n + k) * P:(4 * n + k + 1) * P], W["identb"][:])
                    last.then_inc(f_qT_ps, 1)
                pe.wait_ge(f_qT, at(i, 3, 3))
                for tt in range(TT):
                    for k in range(KF):
                        last = mm(bank(6)[:, tt, :], qT[:, k, tt * P:(tt + 1) * P], w2q[:, k, :],
                                  start=(k == 0), stop=(k == KF - 1))
                last.then_inc(sum_ps, 1)

            def moe(i):
                for tt in range(TT):
                    for k in range(KD):
                        last = mm(ps[:, 6, tt * E:(tt + 1) * E], xT[:, k, tt * P:(tt + 1) * P], W["router"][:, k, :],
                                  start=(k == 0), stop=(k == KD - 1))
                last.then_inc(r_ps, 1)

                def gate_up(c):
                    tt, lo, n = c // 3, c % 3 * 512, min(512, MOE - c % 3 * 512)
                    if c >= 3:
                        pe.wait_ge(moe_h, at(i, 6, c - 2))
                    for b, w in ((0, W["wgate"]), (1, W["wup"])):
                        for k in range(KD):
                            last = mm(ps[:, c % 3 * 2 + b, 0:n], xT[:, k, tt * P:(tt + 1) * P], w[:, k, lo:lo + n],
                                      start=(k == 0), stop=(k == KD - 1))
                    last.then_inc(gu_ps, 1)

                def turn(c):
                    tt, k0, n = c // 3, c % 3 * 4, min(4, KM - c % 3 * 4)
                    pe.wait_ge(moe_h, at(i, 6, c + 1))
                    if c >= 2:
                        pe.wait_ge(moe_hT, at(i, 6, c - 1))
                    for k in range(n):
                        last = tr(bank(6 + c % 2, 4)[:, k, :], mh[:, tt, (k0 + k) * P:(k0 + k + 1) * P], W["ident"][:])
                    last.then_inc(moe_hT_ps, 1)

                for c in range(8):
                    if c < 6:
                        gate_up(c)
                    if c >= 2:
                        turn(c - 2)
                pe.wait_ge(moe_hT, at(i, 6, 6))
                for tt in range(TT):
                    for k in range(KM):
                        last = mm(bank(0)[:, tt, :], mhT[:, k, tt * P:(tt + 1) * P], W["wmoe"][:, k, :],
                                  start=(k == 0), stop=(k == KM - 1))
                last.then_inc(sum_ps, 1)

            with pe.Fori(0, B) as i:
                mamba(i)
                x_transposed(i, 1, 1)
                latent_projections(i)
                attention(i, att0, W["wo0"])
                ffn(i)
                x_transposed(i, 3, 2)
                self_projections(i)
                attention(i, att1, W["wo1"])
                x_transposed(i, 4, 3)
                cross_projections(i)
                attention(i, att2, W["wo2"])
                x_transposed(i, 5, 4)
                moe(i)

        @block.scalar
        def _(act):
            f = nc.scalar.activation

            act.wait_ge(w_first, 16 * len(FIRST))
            act.preload_act_table_set(EXP_LN)
            f(aneg[:], W["alog"][:], ACT.Exp).then_inc(setup_a, 1)
            act.wait_ge(setup_v, 1)

            def rstd_guess_of(i, c, n):
                act.wait_ge(var_ready, at(i, 8, n))
                c.link(f(lnv[:], mv[:, :, 1], ACT.Ln, bias=epsc[:, 0:1]))
                f(rstd[:], lnv[:], ACT.Exp, scale=-0.5).then_inc(rstd_guess, 1)

            def xT_copy(i, nth):
                act.wait_ge(xT_ps, at(i, 4, nth))
                f(xT[:], bank(7), ACT.Copy).then_inc(xT_ready, 1)

            def mamba(i, c):
                for b in range(2):
                    act.wait_ge(xz, at(i, 4, b + 1))
                    f(xin[:, 2 * b:2 * b + 2, TAPS - 1:], bank(b), ACT.Copy).then_inc(xin_sb, 1)
                act.preload_act_table_set(SILU_SET)
                act.wait_ge(xz, at(i, 4, 4))
                f(zs, ps[:, 2:4, :].rearrange("p a b -> p (a b)").rearrange("p (m t) -> p m t", t=T),
                  ACT.Silu).then_inc(silu_z, 1)
                for m in range(M):
                    act.wait_ge(conv_done, at(i, M, m + 1))
                    f(xc[:, m, :], conv[:, m, :], ACT.Silu).then_inc(silu_x, 1)
                act.preload_act_table_set(EXP_LN)
                for n in range(4):
                    act.wait_ge(cnt_ps, at(i, 4, n + 1))
                    f(cnt[0:32, 32 * n:32 * n + 32, :],
                      ps[0:32, 4 + n, :].rearrange("p (q l) -> p q l", l=16), ACT.Copy).then_inc(cnt_sb, 1)
                act.wait_ge(xdbl, at(i, 1, 1))
                f(dtr[0:RANK, :], ps[0:RANK, 4, 0:T], ACT.Copy).then_inc(dtr_sb, 1)
                act.wait_ge(cnt_max, at(i, 1, 1))
                f(cm1, cm1, ACT.Ln).then_inc(cnt_ln, 1)
                act.wait_ge(dt_x, at(i, 1, 1))
                c.link(f(sp_e, sp_x, ACT.Abs))
                c.link(f(sp_e, sp_e, ACT.Exp, scale=-1.0))
                f(sp_l, sp_e, ACT.Ln, bias=onec[:, 0:1]).then_inc(dt_ln, 1)
                act.wait_ge(dt_done, at(i, 1, 1))
                act.wait_ge(pads, at(i, 2, 2))

                def decays(u):
                    m, g = u // STEPS, u % STEPS
                    if u >= 2:
                        act.wait_ge(h_ready, at(i, M * STEPS, u - 1))
                    for n in range(NG):
                        s = g * NG + n
                        last = f(decay[u % 2][:, n, 1:T], dt[:, m, 1:T], ACT.Exp, scale=aneg[:, m, s:s + 1])
                    last.then_inc(decay_ready, 1)

                decays(0)
                decays(1)
                for n in range(8):
                    act.wait_ge(c_ps, at(i, 8, n + 1))
                    f(csb[:, 2 * n:2 * n + 2, :], bank(n % 4), ACT.Copy).then_inc(c_sb, 1)
                for u in range(2, M * STEPS):
                    decays(u)

            def attention(i, c, a):
                def output(u):
                    act.wait_ge(a.pv, at(i, a.UNITS, u + 1))
                    r, qt = a.unit_rows(u), u // (H // 2)
                    f(OT[r, a.out_tile(u), qt * P:(qt + 1) * P], ps[r, 5 + u % 2, 0:P], ACT.Copy).then_inc(a.o, 1)

                for u in range(a.UNITS):
                    if u >= 5:
                        output(u - 5)
                    act.wait_ge(a.rmax, at(i, a.UNITS, u + 1))
                    if u >= 3:
                        act.wait_ge(a.pT_ps, at(i, a.UNITS, u - 2))
                    for j in range(2):
                        src = smask[u % 2][:, j, :] if a.masked else bank(u % 3)[:, j, :]
                        last = f(prob[u % 3][:, j, :], src, ACT.Exp, bias=rmax[:, 2 * u + j:2 * u + j + 1],
                                 scale=-1.0 if a.masked else 1.0, accum_out=rsum[:, 2 * u + j:2 * u + j + 1])
                    last.then_inc(a.probs, 1)
                for u in range(a.UNITS - 5, a.UNITS):
                    output(u)

            with act.Fori(0, B) as i:
                c = Chain(act, a_step, i, A_STEPS)
                mamba(i, c)
                rstd_guess_of(i, c, 1)
                xT_copy(i, 1)
                act.wait_ge(att0.proj, at(i, 4, 1))
                f(ckvT, ps[:, 5, 0:T], ACT.Copy).then_inc(att0.evac, 1)
                act.wait_ge(att0.proj, at(i, 4, 2))
                f(QT[:, 0:4, :], ps[:, 0:2, :].rearrange("p a (b t) -> p (a b) t", t=T), ACT.Copy,
                  scale=0.25).then_inc(att0.evac, 1)
                act.wait_ge(att0.proj, at(i, 4, 3))
                for g in range(2):
                    last = f(KT[:, 4 * g:4 * g + 4, :], ps[:, 2:4, :].rearrange("p a (b t) -> p (a b) t", t=T),
                             ACT.Copy, scale=W["group"][:, g:g + 1])
                last.then_inc(att0.evac, 1)
                attention(i, c, att0)
                rstd_guess_of(i, c, 2)
                rstd_guess_of(i, c, 3)
                act.wait_ge(f_qT_ps, at(i, 3, 1))
                f(qT[:, 0:KD, :], ps[:, 6, :].bitcast(BF16).rearrange("p (k t) -> p k t", t=T)[:, 0:KD, :],
                  ACT.Copy).then_inc(f_qT, 1)
                act.preload_act_table_set(GELU_SET)
                for tt in range(TT):
                    act.wait_ge(f_h, at(i, TT, tt + 1))
                    f(fh[:, tt, :], fh[:, tt, :], ACT.Gelu).then_inc(f_gelu, 1)
                act.preload_act_table_set(EXP_LN)
                rstd_guess_of(i, c, 4)
                for n in range(2):
                    act.wait_ge(f_qT_ps, at(i, 3, n + 2))
                    f(qT[:, 4 * n:4 * n + 4, :], ps[:, 4 + n, :].bitcast(BF16).rearrange("p (k t) -> p k t", t=T),
                      ACT.Copy).then_inc(f_qT, 1)
                rstd_guess_of(i, c, 5)
                xT_copy(i, 2)
                act.wait_ge(att1.proj, at(i, 3, 2))
                for g in range(2):
                    for t in range(4):
                        last = f(KT[:, 4 * g + t, :], bank(2 + t // 2)[:, t % 2, :], ACT.Identity,
                                 bias=kbh[:, g, t:t + 1], scale=hmk[:, g, t:t + 1])
                last.then_inc(att1.evac, 1)
                attention(i, c, att1)
                rstd_guess_of(i, c, 6)
                xT_copy(i, 3)
                for n in range(4):
                    act.wait_ge(att2.proj, at(i, 12, 5 + n))
                    f(KT[:, 2 * n:2 * n + 2, :], bank(3 + n), ACT.Copy).then_inc(att2.evac, 1)
                attention(i, c, att2)
                rstd_guess_of(i, c, 7)
                xT_copy(i, 4)
                for tt in range(TT):
                    act.wait_ge(r_max, at(i, 1, 1))
                    last = f(route[:, 0, tt, :], ps[:, 6, tt * E:(tt + 1) * E], ACT.Exp, bias=rs2[:, 0, tt:tt + 1])
                last.then_inc(r_exp, 1)
                act.preload_act_table_set(SILU_SET)

                def moe_turned(k):
                    tt, k0, n = k // 3, k % 3 * 4, min(4, KM - k % 3 * 4)
                    act.wait_ge(moe_hT_ps, at(i, 6, k + 1))
                    f(mhT[:, k0:k0 + n, tt * P:(tt + 1) * P], bank(6 + k % 2, 4)[:, 0:n, :],
                      ACT.Copy).then_inc(moe_hT, 1)

                for k in range(8):
                    if k < 6:
                        tt, lo, n = k // 3, k % 3 * 512, min(512, MOE - k % 3 * 512)
                        act.wait_ge(gu_ps, at(i, 6, k + 1))
                        f(sg[:, tt, lo:lo + n], ps[:, k % 3 * 2, 0:n], ACT.Silu).then_inc(gu_silu, 1)
                    if k >= 2:
                        moe_turned(k - 2)
                act.preload_act_table_set(EXP_LN)
                rstd_guess_of(i, c, 8)
                c.close()

        @block.gpsimd
        def _(pool):
            with pool.Fori(0, B) as i:
                pool.wait_ge(c_sb, at(i, 8, 8))
                pool.wait_ge(stored, at(i, 16, 16))
                for u in range(M * STEPS):
                    pool.wait_ge(h_ready, at(i, M * STEPS, u + 1))
                    if u >= 2:
                        pool.wait_ge(y_ready, at(i, M * STEPS, u - 1))
                    g = u % STEPS
                    nc.gpsimd.tensor_tensor(hc[u % 2], hbuf[u % 2], csb[:, g * NG:(g + 1) * NG, :],
                                            ALU.mult).then_inc(hc_ready, 1)
                for a in (att0, att1, att2):
                    for u in range(a.UNITS):
                        pool.wait_ge(a.inv, at(i, a.UNITS, u + 1))
                        nc.gpsimd.tensor_tensor(prob[u % 3], prob[u % 3],
                                                rinv[:, 2 * u:2 * u + 2].unsqueeze(2).to_broadcast([P, 2, T]),
                                                ALU.mult).then_inc(a.norm, 1)

        @block.vector
        def _(v):
            tt_, ts, stt, cp = nc.vector.tensor_tensor, nc.vector.tensor_scalar, nc.vector.scalar_tensor_tensor, nc.vector.tensor_copy

            nc.vector.memset(epsc[:], EPS).then_inc(setup_v, 1)
            v.wait_ge(staged, 32)
            nc.vector.tensor_reduce(wscale[:, 0:1], wst.rearrange("p a b -> p (a b)"), AX, ALU.add,
                                    apply_absolute_value=True)
            nc.vector.tensor_reduce(wscale[:, 1:2], wst2.rearrange("p a b -> p (a b)"), AX, ALU.add,
                                    apply_absolute_value=True).then_inc(setup_v, 1)
            v.wait_ge(setup_a, 1)
            ts(aneg[:], aneg[:], -1.0, None, ALU.mult).then_inc(setup_v, 1)
            v.wait_ge(setup_t, 1)
            ts(wscale[:, 2:4], ps[:, 0, 0:2], 1.0 / (D * FF), 1e-5, ALU.mult, ALU.max).then_inc(setup_v, 1)
            v.wait_ge(setup_v, 4)
            nc.vector.reciprocal(wscale[:, 4:6], wscale[:, 2:4]).then_inc(setup_v, 1)
            v.wait_ge(setup_v, 5)
            n = 5
            flat = [(wst, wscale[:, 4:5], w1q[:].rearrange("p a b -> p (a b)")),
                    (wst2, wscale[:, 5:6], w2q[:].rearrange("p a b -> p (a b)"))]
            for w, inv, q in flat:
                w = w.rearrange("p a b -> p (a b)")
                for o, s1, s2, op0, op1 in ((w, inv, ROUND, ALU.mult, ALU.add),
                                            (w, -ROUND, -1.0, ALU.add, ALU.max),
                                            (q, 1.0, None, ALU.min, ALU.bypass)):
                    ts(o, w, s1, s2, op0, op1).then_inc(setup_v, 1)
                    n += 1
                    v.wait_ge(setup_v, n)
            for g in range(2):
                ts(hmk[:, g, :], W["hm1"][:], W["group"][:, g:g + 1], None, ALU.mult).then_inc(setup_v, 1)
            ts(hmq[:], W["hm1"][:], 0.25, None, ALU.mult).then_inc(setup_v, 1)
            v.wait_ge(setup_v, n + 3)
            for g in range(2):
                tt_(kbh[:, g, :], W["kb1"][:], hmk[:, g, :], ALU.mult).then_inc(setup_v, 1)
            v.wait_ge(setup_v, n + 5)
            nc.vector.memset(onec[:], 1.0).then_inc(batch_done, 1)

            def normalised(i, c, n, src, dst, width):
                parts = max(1, width // 512)
                for tt in range(TT):
                    for p in range(parts):
                        w = width // parts
                        c.did(nc.vector.bn_stats(stats[:, tt, p, :], src[:, tt, p * w:(p + 1) * w]))
                c.settle()
                nc.vector.memset(spare[:, n:n + 1], 0.0)
                for tt in range(TT):
                    last = nc.vector.bn_aggr(mv[:, tt, :], stats[:, tt, 0:parts, :].rearrange("p a b -> p (a b)"))
                last.then_inc(var_ready, 1)
                v.wait_ge(rstd_guess, at(i, 8, n))
                c.link(stt(nt[:], mv[:, :, 1], EPS, rstd[:], ALU.add, ALU.mult))
                c.link(stt(nt[:], nt[:], -0.5, rstd[:], ALU.mult, ALU.mult))
                c.link(stt(rstd[:], nt[:], 1.5, rstd[:], ALU.add, ALU.mult))
                for tt in range(TT):
                    last = ts(dst[:, tt, :], src[:, tt, :], mv[:, tt, 0:1], rstd[:, tt:tt + 1],
                              ALU.subtract, ALU.mult)
                return last

            def residual(i, c, n, b, addend, dst, done, dequant=None):
                v.wait_ge(sum_ps, at(i, 6, n))
                tt_(res, bank(b), addend, ALU.add).then_inc(sum_read, 1)
                v.wait_ge(sum_read, at(i, 6, n))
                return res

            def quantised(i, c, src, width, wcol):
                c.link(nc.vector.tensor_reduce(small[:, 0, :], src, AX, ALU.max, apply_absolute_value=True))
                c.link(ts(small[:, 1, :], small[:, 0, :], 1e-5, None, ALU.max))
                c.did(nc.vector.reciprocal(small[:, 2, :], small[:, 1, :]))
                c.did(ts(small[:, 4, :], small[:, 1, :], 1.0 / 127.0, wscale[:, wcol:wcol + 1], ALU.mult, ALU.mult))
                c.settle()
                c.link(ts(small[:, 3, :], small[:, 2, :], 127.0, None, ALU.mult))
                for tt in range(TT):
                    c.did(ts(src[:, tt, :], src[:, tt, :], small[:, 3, tt:tt + 1], -128.0, ALU.mult, ALU.max))
                c.settle()
                c.did(ts(src, src, 127.0, ROUND, ALU.min, ALU.add))
                c.settle()
                return ts(qb[:, :, 0:width], src, -ROUND, None, ALU.add)

            def mamba(i, c):
                v.wait_ge(batch_done, i + 1)
                v.wait_ge(loaded, at(i, 48, 48))
                cp(ix[0], idx[:]).then_inc(idx_read, 1)
                v.wait_ge(idx_read, at(i, 1, 1))
                c.link(ts(ix[1], ix[0], 0.0, float(T), ALU.is_lt, ALU.mult))
                c.link(tt_(ix[2], ix[0], ix[1], ALU.add))
                c.link(ts(ixi[3], ix[2], 0.0, float(T - 1), ALU.max, ALU.min))
                c.did(ts(ixi[4], ixi[3], 4, None, ALU.logical_shift_right))
                c.did(ts(ixi[5], ixi[3], 15, None, ALU.bitwise_and))
                c.settle()
                c.did(ts(hib, ixi[4], W["half"][:, 0:1], None, ALU.add))
                c.did(cp(lob, ixi[5]))
                c.settle()
                for o, a, n in ((oh_hi, hib, 32), (oh_lo, lob, 16)):
                    tt_(o, a.unsqueeze(2).to_broadcast([P, P, n]),
                        W["iota"][:, 0:n].unsqueeze(1).to_broadcast([P, P, n]), ALU.is_equal).then_inc(onehot, 1)
                c.link(nc.vector.memset(xin[:, :, 0:TAPS - 1], 0.0))
                for m in range(M):
                    v.wait_ge(xin_sb, at(i, 2, m // 2 + 1))
                    c.did(ts(conv[:, m, :], xin[:, m, 0:T], W["convw"][:, m, 0:1], W["convb"][:, m:m + 1],
                             ALU.mult, ALU.add))
                for k in range(1, TAPS):
                    c.settle()
                    for m in range(M):
                        ins = stt(conv[:, m, :], xin[:, m, k:k + T], W["convw"][:, m, k:k + 1], conv[:, m, :],
                                  ALU.mult, ALU.add)
                        if k < TAPS - 1:
                            c.did(ins)
                        else:
                            ins.then_inc(conv_done, 1)
                v.wait_ge(cntT, at(i, 1, 1))
                for s in range(2):
                    nc.vector.memset(decay[s][:, :, 0:1], 0.0).then_inc(pads, 1)
                counts = ps[:, 6, 0:256].bitcast(BF16).rearrange("q (l t h) -> q t h l", l=16, t=TT)
                as4 = lambda ap: ap.rearrange("q t (h l) -> q t h l", l=16)
                for t in range(TT):
                    ts(as4(cm1)[:, t], counts[:, t], 1.0, None, ALU.max)
                    last = ts(as4(cm0)[:, t], counts[:, t], 0.0, MASKED, ALU.is_equal, ALU.mult)
                last.then_inc(cnt_max, 1)
                v.wait_ge(xdbl, at(i, 1, 1))
                c.link(cp(bcs[0:96, :], ps[0:96, 5, 0:T]))
                c.link(tt_(br1[0:96, :], ps[0:96, 5, 0:T], bcs[0:96, :], ALU.subtract))
                c.link(cp(bmid[0:96, :], br1[0:96, :]))
                cp(bcs[32:64, :], bmid[32:64, :])
                tt_(bcs[64:96, :], br1[64:96, :], bmid[64:96, :], ALU.subtract).then_inc(bc_split, 1)
                for m in range(M):
                    v.wait_ge(dt_ps, at(i, 2, m // 2 + 1))
                    last = ts(sp_x[:, m, :], bank(6 + m // 2)[:, m % 2, :], W["bdt"][:, m:m + 1], None, ALU.add)
                last.then_inc(dt_x, 1)
                v.wait_ge(cnt_ln, at(i, 1, 1))
                c.did(tt_(mask[:], cm1, cm0, ALU.add))
                v.wait_ge(dt_ln, at(i, 1, 1))
                c.link(ts(dt, sp_e, 1.0, None, ALU.add))
                c.did(stt(dtx, dt, 1.0, sp_e, ALU.subtract, ALU.subtract))
                c.did(stt(sp_x, sp_x, 0.0, sp_l, ALU.max, ALU.add))
                c.settle()
                tt_(dt, sp_x, dtx, ALU.subtract).then_inc(dt_done, 1)
                v.wait_ge(dt_done, at(i, 1, 1))
                c.link(tt_(dtx, dt, xc, ALU.mult))

                def gate(m):
                    v.wait_ge(y_ready, at(i, M * STEPS, STEPS * (m + 1)))
                    c.link(stt(yT[:, m, :], xc[:, m, :], W["dp"][:, m:m + 1], ps[:, 4 + m % 2, 0:T], ALU.mult, ALU.add))
                    tt_(yT[:, m, :], yT[:, m, :], zs[:, m, :], ALU.mult).then_inc(y_done, 1)

                for u in range(M * STEPS):
                    m = u // STEPS
                    v.wait_ge(b_ps, at(i, M * STEPS, u + 1))
                    if u >= 2:
                        v.wait_ge(hc_ready, at(i, M * STEPS, u - 1))
                    b = ps[:, u % 2 * 2:u % 2 * 2 + 2, :].rearrange("p a (b t) -> p (a b) t", t=T)
                    tt_(hbuf[u % 2], dtx[:, m, :].unsqueeze(1).to_broadcast([P, NG, T]), b, ALU.mult).then_inc(b_used, 1)
                    v.wait_ge(b_used, at(i, M * STEPS, u + 1))
                    v.wait_ge(decay_ready, at(i, M * STEPS, u + 1))
                    flat = lambda ap: ap.rearrange("p a b -> p (a b)")
                    nc.vector.tensor_tensor_scan(flat(hbuf[u % 2]), flat(decay[u % 2]), flat(hbuf[u % 2]), 0.0,
                                                 ALU.mult, ALU.add).then_inc(h_ready, 1)
                    if u % STEPS == 2 and m >= 1:
                        gate(m - 1)
                gate(M - 1)

            def attention(i, c, a):
                for u in range(a.UNITS + 3):
                    if u < a.UNITS:
                        qt = u // (H // 2)
                        v.wait_ge(a.s_ps, at(i, a.UNITS, u + 1))
                        if a.masked:
                            if u >= 2:
                                v.wait_ge(a.probs, at(i, a.UNITS, u - 1))
                            nc.vector.memset(spare[:, 9 + u:10 + u], 0.0)
                            for j in range(2):
                                last = nc.vector.tensor_tensor_reduce(
                                    smask[u % 2][:, j, :], bank(u % 3)[:, j, :], mask[:, qt, :], -1.0, HUGE,
                                    ALU.add, ALU.min, rmax[:, 2 * u + j:2 * u + j + 1])
                        else:
                            last = nc.vector.tensor_reduce(rmax[:, 2 * u:2 * u + 2], bank(u % 3), AX, ALU.max,
                                                           negate=True)
                        last.then_inc(a.rmax, 1)
                    if 0 <= u - 1 < a.UNITS:
                        w = u - 1
                        v.wait_ge(a.probs, at(i, a.UNITS, w + 1))
                        nc.vector.reciprocal(rinv[:, 2 * w:2 * w + 2], rsum[:, 2 * w:2 * w + 2]).then_inc(a.inv, 1)
                    if 0 <= u - 3:
                        w = u - 3
                        v.wait_ge(a.pT_ps, at(i, a.UNITS, w + 1))
                        if w >= 2:
                            v.wait_ge(a.pv, at(i, a.UNITS, w - 1))
                        cp(probT[w % 2], bank(3 + w % 2, 4)).then_inc(a.pT, 1)

            def ffn(i, c):
                hn = fq[:, :, 0:D]
                c.did(normalised(i, c, 3, x[:], hn, D))
                c.settle()
                bc = lambda w: w.unsqueeze(1).to_broadcast([P, TT, w.shape[1]])
                c.link(tt_(hn, hn, bc(W["ln1g"][:]), ALU.mult))
                c.link(tt_(hn, hn, bc(W["ln1b"][:]), ALU.add))
                quantised(i, c, hn, D, 2).then_inc(f_q, 1)
                v.wait_ge(rows_loaded, at(i, 48, 48))
                for tt in range(TT):
                    v.wait_ge(f_h_ps, at(i, TT, tt + 1))
                    stt(fh[:, tt, :], ps[:, 2 * tt:2 * tt + 2, :].rearrange("p a b -> p (a b)"),
                        small[:, 4, tt:tt + 1], fb1, ALU.mult, ALU.add).then_inc(f_h, 1)
                v.wait_ge(f_gelu, at(i, TT, 2))
                c.did(normalised(i, c, 4, fh, fq, FF))
                c.settle()
                c.link(tt_(fq, fq, bc(ln2g), ALU.mult))
                c.link(tt_(fq, fq, bc(ln2b), ALU.add))
                quantised(i, c, fq, FF, 3).then_inc(f_q, 1)
                c.link(tt_(x[:], x[:], bc(W["fb2"][:]), ALU.add))
                v.wait_ge(sum_ps, at(i, 6, 3))
                for tt in range(TT):
                    last = stt(res[:, tt, :], bank(6)[:, tt, :], small[:, 4, tt:tt + 1], x[:, tt, :], ALU.mult, ALU.add)
                last.then_inc(sum_read, 1)
                v.wait_ge(sum_read, at(i, 6, 3))

            def moe(i, c):
                v.wait_ge(r_ps, at(i, 1, 1))
                logits = ps[:, 6, 0:TT * E].rearrange("p (t e) -> p t e", e=E)
                nc.vector.tensor_reduce(rs2[:, 0, :], logits, AX, ALU.max, negate=True).then_inc(r_max, 1)
                v.wait_ge(r_exp, at(i, 1, 1))
                c.link(nc.vector.tensor_reduce(rs2[:, 1, :], route[:, 0], AX, ALU.add))
                c.link(nc.vector.reciprocal(rs2[:, 2, :], rs2[:, 1, :]))
                c.link(tt_(route[:, 1], route[:, 0], rs2[:, 2, :].unsqueeze(2).to_broadcast([P, TT, E]), ALU.mult))
                for tt in range(TT):
                    mine = route[:, 1, tt, :].unsqueeze(2).to_broadcast([P, E, E])
                    other = route[:, 1, tt, :].unsqueeze(1).to_broadcast([P, E, E])
                    c.did(tt_(rcmp[:, 0, tt], other, mine, ALU.is_gt))
                    c.did(tt_(rcmp[:, 1, tt], other, mine, ALU.is_equal))
                c.settle()
                for tt in range(TT):
                    c.did(tt_(rcmp[:, 1, tt], rcmp[:, 1, tt], W["tri"][:], ALU.mult))
                c.settle()
                c.link(tt_(rcmp[:, 0].rearrange("p t a b -> p (t a b)"), rcmp[:, 0].rearrange("p t a b -> p (t a b)"),
                           rcmp[:, 1].rearrange("p t a b -> p (t a b)"), ALU.add))
                c.link(nc.vector.tensor_reduce(route[:, 2].rearrange("p t e -> p (t e)"),
                                               rcmp[:, 0].rearrange("p t a b -> p (t a) b"), AX, ALU.add))
                c.link(stt(route[:, 3], route[:, 2], float(TOPK), route[:, 1], ALU.is_lt, ALU.mult))
                for k in range(6):
                    tt, lo, n = k // 3, k % 3 * 512, min(512, MOE - k % 3 * 512)
                    v.wait_ge(gu_silu, at(i, 6, k + 1))
                    up = ps[:, k % 3 * 2 + 1, 0:n]
                    if n == 512:
                        for e in range(4):
                            w = route[:, 3, tt, lo // FE + e:lo // FE + e + 1]
                            last = stt(mh[:, tt, lo + e * FE:lo + (e + 1) * FE], sg[:, tt, lo + e * FE:lo + (e + 1) * FE], w,
                                       up[:, e * FE:(e + 1) * FE], ALU.mult, ALU.mult)
                    else:
                        last = tt_(mh[:, tt, lo:lo + n], sg[:, tt, lo:lo + n], up, ALU.mult)
                    last.then_inc(moe_h, 1)

            with v.Fori(0, B) as i:
                c = Chain(v, v_step, i, V_STEPS)
                bc = lambda w: w.unsqueeze(1).to_broadcast([P, TT, D])
                mamba(i, c)
                residual(i, c, 1, 6, x_in[:], None, None)
                normalised(i, c, 1, res, x, D).then_inc(x_ready, 1)
                v.wait_ge(att0.proj, at(i, 4, 4))
                nc.vector.memset(VP[:, :, :, 16:32], 0.0)
                cp(VP[:, :, :, 0:16], bank(4).rearrange("p t (h d) -> p t h d", d=16)).then_inc(att0.vevac, 1)
                attention(i, c, att0)
                residual(i, c, 2, 7, x[:], None, None)
                normalised(i, c, 2, res, x, D).then_inc(x_ready, 1)
                v.wait_ge(x_ready, at(i, 5, 2))
                ffn(i, c)
                normalised(i, c, 5, res, x, D).then_inc(x_ready, 1)
                for t in range(4):
                    v.wait_ge(att1.proj, at(i, 3, 1))
                    last = ts(QT[:, t, :], bank(t // 2)[:, t % 2, :], W["qb1"][:, t:t + 1], hmq[:, t:t + 1],
                              ALU.add, ALU.mult)
                last.then_inc(att1.vevac, 1)
                v.wait_ge(att1.proj, at(i, 3, 3))
                c.link(tt_(ckvT2, bank(4), bc(W["vb1"][:]), ALU.add))
                nc.vector.memset(VP[:, :, :, 16:32], 0.0)
                for t in range(TT):
                    last = tt_(VP[:, t, :, 0:16], ckvT2[:, t, :].rearrange("p (h d) -> p h d", d=16),
                               W["hmv1"][:].rearrange("p (h d) -> p h d", d=16), ALU.mult)
                last.then_inc(att1.vevac, 1)
                attention(i, c, att1)
                c.link(tt_(x[:], x[:], bc(W["ob1"][:]), ALU.add))
                residual(i, c, 4, 7, x[:], None, None)
                normalised(i, c, 6, res, x, D).then_inc(x_ready, 1)
                for n in range(4):
                    v.wait_ge(att2.proj, at(i, 12, n + 1))
                    ts(QT[:, 2 * n:2 * n + 2, :], bank((0, 1, 2, 7)[n]), 0.125, None, ALU.mult).then_inc(att2.vevac, 1)
                for n in range(4):
                    v.wait_ge(att2.proj, at(i, 12, n + 9))
                    cp(VV[:, n // 2, n % 2 * 512:(n % 2 + 1) * 512], ps[:, (0, 1, 2, 7)[n], :]).then_inc(att2.vevac, 1)
                attention(i, c, att2)
                c.link(tt_(x[:], x[:], bc(W["ob2"][:]), ALU.add))
                residual(i, c, 5, 7, x[:], None, None)
                normalised(i, c, 7, res, x, D).then_inc(x_ready, 1)
                moe(i, c)
                residual(i, c, 6, 0, x[:], None, None)
                v.wait_ge(stored, at(i, 16, 16))
                normalised(i, c, 8, res, x_out, D).then_inc(batch_done, 1)
                c.close()


def layouts(a):
    n = {k: np.asarray(v) for k, v in a.items()}

    def tiles(w):
        return np.ascontiguousarray(w.reshape(-1, P, w.shape[1]).transpose(1, 0, 2))

    def columns(w):
        return np.ascontiguousarray(w.reshape(-1, P).T)

    def rows(w):
        return np.ascontiguousarray(np.broadcast_to(w.reshape(1, -1), (P, w.size)))

    def heads16(w):
        o = np.zeros((w.shape[0], 4, 4, 32), w.dtype)
        o[:, :, :, 0:16] = w.reshape(-1, 4, 4, 16).transpose(0, 2, 1, 3)
        return o.reshape(w.shape[0], 512)

    def pad32(w):
        o = np.zeros((H, 32, w.shape[1]), w.dtype)
        o[:, 0:16] = w.reshape(H, 16, -1)
        return o.reshape(H * 32, -1)

    def heads64(w):
        return w.reshape(-1, 2, 8, 64).transpose(0, 2, 1, 3).reshape(-1, 1024)

    x = n["x"]
    wx = n["L0_attn_W_xproj"]
    qkv = n["L1_attn_qkv_w"].reshape(H, 3, 16, D)
    qkvb = n["L1_attn_qkv_b"].reshape(H, 3, 16)
    hm = np.repeat(n["L1_attn_head_mask"], 16)
    per_head = lambda w: columns(heads16(w.reshape(1, -1)).reshape(-1))
    kup = n["L0_xattn_W_kv_up"]
    experts = lambda w: w.transpose(1, 0, 2).reshape(D, E * FE)
    sel = np.zeros((96, 32), np.float32)
    for r in range(3):
        sel[32 * r + np.arange(32), np.arange(32)] = 1
    bf = np.dtype(mybir.dt.np(BF16))
    tri = np.zeros((P, E, E), np.float32)
    for e in range(E):
        tri[:, e, :e] = 1
    return {
        "x": x.reshape(B, TT, P, D),
        "xT": np.ascontiguousarray(x.transpose(0, 2, 1)).reshape(B, KD, P, T),
        "ctxT": np.ascontiguousarray(n["ctx_1024"].transpose(0, 2, 1)).reshape(B, KD, P, T),
        "idx": np.ascontiguousarray(n["itok_BxSx64_0_2047"].reshape(B, TT, P, SEL).transpose(0, 1, 3, 2)).reshape(B, P, P),
        "w1": tiles(n["L0_ffn_w1"].T), "w2": tiles(n["L0_ffn_w2"].T),
        "win": tiles(n["L0_attn_W_in"]), "wxd": tiles(wx[:, :RANK]),
        "wbc": tiles(np.concatenate([wx[:, RANK:]] * 3, 1)),
        "wdt": n["L0_attn_W_dt"], "wout": tiles(n["L0_attn_W_out"]),
        "convw": tiles(n["L0_attn_conv_w"]), "convb": columns(n["L0_attn_conv_b"]),
        "bdt": columns(n["L0_attn_b_dt"]), "alog": tiles(n["L0_attn_A_log"]), "dp": columns(n["L0_attn_Dp"]),
        "ident": np.eye(P, dtype=np.float32), "identb": np.eye(P, dtype=np.float32).astype(bf), "sel": sel.astype(bf),
        "iota": np.tile(np.arange(32, dtype=np.float32), (P, 1)).astype(bf),
        "group": np.tile(np.repeat(np.eye(2, dtype=np.float32), 32, 0), (2, 1)),
        "half": np.repeat(np.float32([0, 16]), SEL).reshape(P, 1), "ones": np.ones((P, P), np.float32), "tri": tri,
        "wq0": tiles(heads16(n["L0_xattn_W_q"].T)), "wdown0": tiles(n["L0_xattn_W_kv_down"].T),
        "wk0": heads16(kup[:D].T), "wv0": np.ascontiguousarray(kup[D:].T), "wo0": tiles(pad32(n["L0_xattn_W_out"].T)),
        "ln1g": rows(n["L0_ffn_ln1_g"]), "ln1b": rows(n["L0_ffn_ln1_b"]), "fb1": rows(n["L0_ffn_b1"]),
        "ln2g": rows(n["L0_ffn_ln2_g"]), "ln2b": rows(n["L0_ffn_ln2_b"]), "fb2": rows(n["L0_ffn_b2"]),
        "wq1": tiles(heads16(qkv[:, 0].reshape(D, D).T)), "wk1": tiles(heads16(qkv[:, 1].reshape(D, D).T)),
        "wv1": tiles(qkv[:, 2].reshape(D, D).T),
        "qb1": per_head(qkvb[:, 0]), "kb1": per_head(qkvb[:, 1]), "hm1": per_head(hm),
        "vb1": rows(qkvb[:, 2]), "hmv1": rows(hm),
        "wo1": tiles(pad32(n["L1_attn_fc_w"].T)), "ob1": rows(n["L1_attn_fc_b"]),
        "wq2": tiles(heads64(n["L1_xattn_Wq"])), "wk2": tiles(heads64(n["L1_xattn_Wkv"][:, :1024])),
        "wv2": tiles(n["L1_xattn_Wkv"][:, 1024:]), "wo2": tiles(n["L1_xattn_Wo"]), "ob2": rows(n["L1_xattn_bo"]),
        "router": tiles(n["L1_ffn_router_w"]),
        "wgate": tiles(np.concatenate([experts(n["L1_ffn_w_gate"]), n["L1_ffn_ws_gate"]], 1)),
        "wup": tiles(np.concatenate([experts(n["L1_ffn_w_up"]), n["L1_ffn_ws_up"]], 1)),
        "wmoe": tiles(np.concatenate([n["L1_ffn_w_down"].reshape(E * FE, D), n["L1_ffn_ws_down"]], 0)),
    }


def kernel(**inputs):
    from concourse import bacc
    from concourse.bass_utils import run_bass_kernel_spmd

    nc = bacc.Bacc("TRN2", target_bir_lowering=False, num_devices=1)
    arrays, dram = {}, {}
    for name, a in layouts(inputs).items():
        a = np.ascontiguousarray(a)
        arrays[f"in_{name}"] = a
        dram[name] = nc.dram_tensor(f"in_{name}", a.shape, mybir.dt.from_np(a.dtype), kind="ExternalInput").ap()
    out = nc.dram_tensor("out_x", (B, TT, P, D), F32, kind="ExternalOutput").ap()
    build(nc, dram, out)
    r = run_bass_kernel_spmd(nc, [arrays], core_ids=[0])
    return r.results[0]["out_x"].reshape(B, T, D)
```

```python
from contextlib import ExitStack

import numpy as np

import concourse.bass as bass
from concourse import mybir

F32 = mybir.dt.float32
BF16 = mybir.dt.bfloat16
I32 = mybir.dt.int32
ALU = mybir.AluOpType
ACT = mybir.ActivationFunctionType
AX = mybir.AxisListType.X

P = 128
B, T, D = 16, 256, 256
TT = T // P
KD = D // P
DI, NS, TAPS, RANK = 512, 16, 4, 64
M = DI // P
NG = 4
STEPS = NS // NG
SEL = 64
H = 16
FF = 1024
KF = FF // P
E, TOPK, FE = 8, 6, 128
MOE = E * FE + 256
KM = MOE // P
EPS = 1e-5
ROUND = 12582912.0
MASKED = -1e30
HUGE = 3e38
EXP_LN = "natural_log_exp_and_others"
SILU_SET = "silu_and_others"
GELU_SET = "gelu_and_others"


def at(i, per, n):
    return i * per + n


class Chain:

    def __init__(self, eng, sem, i, per):
        self.eng, self.sem, self.i, self.per, self.n = eng, sem, i, per, 0

    def did(self, ins):
        self.n += 1
        return ins.then_inc(self.sem, 1)

    def settle(self):
        self.eng.wait_ge(self.sem, at(self.i, self.per, self.n))

    def link(self, ins):
        self.did(ins)
        self.settle()

    def close(self):
        assert self.n == self.per, f"steps per sequence: {self.n}, stated {self.per}"


V_STEPS = 116
A_STEPS = 12
CHOICES_STEPS = 8

CONST_INPUTS = [
    ("win", (P, KD, 2 * DI), F32), ("wxd", (P, M, RANK), F32), ("wbc", (P, M, 96), F32),
    ("wdt", (RANK, DI), F32), ("wout", (P, M, D), F32),
    ("convw", (P, M, TAPS), F32), ("convb", (P, M), F32), ("bdt", (P, M), F32),
    ("alog", (P, M, NS), F32), ("dp", (P, M), F32),
    ("ident", (P, P), F32), ("identb", (P, P), BF16), ("sel", (96, 32), BF16),
    ("iota", (P, 32), BF16), ("group", (P, 4), F32), ("side", (P, 2), F32), ("half", (P, 1), F32), ("ones", (P, P), F32), ("tri", (P, E, E), F32),
    ("wq0", (P, KD, 512), F32), ("wdown0", (P, KD, P), F32), ("wk0", (P, 512), F32),
    ("wv0", (P, D), F32), ("wo0", (P, 4, D), F32),
    ("ln1g", (P, D), F32), ("ln1b", (P, D), F32), ("fb2", (P, D), F32),
    ("wq1", (P, KD, 512), F32), ("wk1", (P, KD, 512), F32), ("wv1", (P, KD, D), F32),
    ("qb1", (P, 4), F32), ("kb1", (P, 4), F32), ("hm1", (P, 4), F32),
    ("vb1", (P, D), F32), ("hmv1", (P, D), F32), ("wo1", (P, 4, D), F32), ("ob1", (P, D), F32),
    ("wq2", (P, KD, 1024), F32), ("wk2", (P, KD, 1024), F32), ("wv2", (P, KD, 1024), F32),
    ("wo2", (P, 8, D), F32), ("ob2", (P, D), F32),
    ("router", (P, KD, E), F32), ("wgate", (P, KD, MOE), F32), ("wup", (P, KD, MOE), F32),
    ("wmoe", (P, KM, D), F32),
]


def build(nc, dram, out):
    ctx = ExitStack()
    with ctx:
        def sb(name, shape, dt=F32):
            return ctx.enter_context(nc.sbuf_tensor(name, list(shape), dt))

        def sem(name):
            return ctx.enter_context(nc.semaphore(name))

        W = {name: sb(name, shape, dt) for name, shape, dt in CONST_INPUTS}
        aneg = sb("aneg", (P, M, NS))
        w1q = sb("w1q", (P, KD, FF), BF16)
        w2q = sb("w2q", (P, KF, D), BF16)
        wscale = sb("wscale", (P, 8))
        epsc = sb("epsc", (P, 1))
        onec = sb("onec", (P, 1))

        x_in = sb("x_in", (P, TT, D))
        xT_in = sb("xT_in", (P, KD, T))
        ctxT = sb("ctxT", (P, KD, T))
        idx = sb("idx", (P, P), I32)
        x = sb("x", (P, TT, D))
        xT = sb("xT", (P, KD, T))
        res_out = sb("res_out", (P, 2, TT, D))
        res, x_out = res_out[:, 0], res_out[:, 1]
        mask = sb("mask", (P, TT, T))
        stats = sb("stats", (P, TT, 2, 6))
        mv = sb("mv", (P, TT, 2))
        lnv = sb("lnv", (P, TT))
        rstd = sb("rstd", (P, TT))
        nt = sb("nt", (P, TT))
        small = sb("small", (P, 8, TT))
        smask1 = sb("smask1", (P, 2, T))
        spare = sb("spare", (P, 9 + TT * H // 2))
        rmax = sb("rmax", (P, TT * H))
        rsum = sb("rsum", (P, TT * H))
        rinv = sb("rinv", (P, TT * H))
        route = sb("route", (P, 6, TT, E))
        rs2 = sb("rs2", (P, 4, TT))
        kbh = sb("kbh", (P, 4, 4))
        hmk = sb("hmk", (P, 4, 4))
        hmq = sb("hmq", (P, 4))

        ARENA = 15120
        arena = sb("arena", (P, ARENA))

        def carve(start, shape, dt=F32):
            n = int(np.prod(shape))
            words = n if dt != BF16 else n // 2
            assert start + words <= ARENA, (start, shape)
            ap = arena[:, start:start + words]
            if dt != F32:
                ap = ap.bitcast(dt)
            if len(shape) > 1:
                names = "abcd"[:len(shape)]
                sizes = {c: s for c, s in zip(names, shape)}
                ap = ap.rearrange(f"p ({' '.join(names)}) -> p {' '.join(names)}", **sizes)
            return ap

        PAD = T + TAPS - 1
        xin = carve(0, (M, PAD))
        dtx = carve(0, (M, T))
        conv = carve(1036, (M, T))
        yT = carve(1036, (M, T))
        xc = carve(2060, (M, T))
        zs = carve(3084, (M, T))
        dt = carve(4108, (M, T))
        csb = carve(5132, (NS, T))
        decay = [carve(9228 + 1024 * s, (NG, T)) for s in range(2)]
        hbuf = [carve(11276 + 1024 * s, (NG, T)) for s in range(2)]
        hc = [carve(13324, (NG, T)),
              res_out[:].rearrange("p a t d -> p (a t) d")]
        dtr = carve(14348, (T,))
        bcs = carve(14604, (T,), BF16)
        bmid = carve(14732, (T,), BF16)
        br1 = carve(14860, (T,))
        sp_x = carve(5132, (M, T))
        sp_e = carve(6156, (M, T))
        sp_l = carve(7180, (M, T))
        oh_hi = carve(9228, (P, 32), BF16)
        oh_lo = carve(11276, (P, 16), BF16)
        cnt = carve(12300, (P, 16), BF16)
        cm1 = carve(13324, (TT, T))
        cm0 = carve(13836, (TT, T))
        ix = [carve(8204 + 128 * s, (P,)) for s in range(6)]
        ixi = [a.bitcast(I32) for a in ix]
        hib = carve(8204 + 768, (P,), BF16)
        lob = carve(8204 + 832, (P,), BF16)

        QT = carve(0, (8, T))
        KT16 = carve(1024, (H, T))
        KT64 = [carve(2048, (8, T)), carve(8192, (8, T))]
        VV = carve(4096, (TT, 1024))
        VP = carve(5120, (TT, H, 32))
        OT = carve(6144, (8, T))
        ln2g, ln2b, fb1 = carve(8192, (FF,)), carve(9216, (FF,)), carve(13568, (FF,))
        prob = [carve(start, (2, T)) for start in (10240, 10752, 11264, 14592)]
        probT = [carve(11776 + 512 * s, (4, P)) for s in range(2)]
        smask = [carve(12800, (2, T)), smask1[:, :, :]]
        ckvT = carve(13312, (T,))
        ckvT2 = carve(8192, (TT, D))

        fh = carve(0, (TT, FF))
        fq = carve(2048, (TT, FF))
        qb = carve(4096, (TT, FF), BF16)
        qT = carve(5120, (KF, T), BF16)
        wst = carve(6144, (KD, FF))
        wst2 = carve(8192, (KD, FF))

        sg = carve(0, (TT, MOE))
        mh = carve(2560, (TT, MOE))
        mhT = carve(5120, (KM, T))
        rcmp = carve(7680, (2, TT, E, E))

        ps = ctx.enter_context(nc.psum_tensor("ps", [P, 8, 512], F32))

        def bank(n, a=None):
            ap = ps[:, n, :]
            return ap.rearrange("p (a b) -> p a b", a=a or 2)

        w_first, w_rest, staged = sem("w_first"), sem("w_rest"), sem("staged")
        setup_v, setup_a, setup_t = sem("setup_v"), sem("setup_a"), sem("setup_t")
        batch_done, rows_loaded = sem("batch_done"), sem("rows_loaded")
        loaded, ctx_loaded, stored = sem("loaded"), sem("ctx_loaded"), sem("stored")
        v_step, a_step = sem("v_step"), sem("a_step")
        xz = sem("xz")
        xin_sb = sem("xin_sb")
        conv_done = sem("conv_done")
        silu_x, silu_z = sem("silu_x"), sem("silu_z")
        onehot = sem("onehot")
        idx_loaded, choices_step, pads = sem("idx_loaded"), sem("choices_step"), sem("pads")
        cnt_ps, cnt_sb, cntT, cnt_max, cnt_ln = sem("cnt_ps"), sem("cnt_sb"), sem("cntT"), sem("cnt_max"), sem("cnt_ln")
        xdbl, dtr_sb, bc_split = sem("xdbl"), sem("dtr_sb"), sem("bc_split")
        dt_ps, dt_x, dt_ln, dt_done = sem("dt_ps"), sem("dt_x"), sem("dt_ln"), sem("dt_done")
        c_ps, c_sb = sem("c_ps"), sem("c_sb")
        b_ps, b_used, decay_ready, h_ready, hc_ready, y_ready, y_done = (
            sem("b_ps"), sem("b_used"), sem("decay_ready"), sem("h_ready"), sem("hc_ready"),
            sem("y_ready"), sem("y_done"))
        sum_ps, sum_read = sem("sum_ps"), sem("sum_read")
        x_ready, xT_ps, xT_ready = sem("x_ready"), sem("xT_ps"), sem("xT_ready")
        var_ready, rstd_guess = sem("var_ready"), sem("rstd_guess")
        f_q, f_qT_ps, f_qT, f_h_ps, f_h, f_gelu = (
            sem("f_q"), sem("f_qT_ps"), sem("f_qT"), sem("f_h_ps"), sem("f_h"), sem("f_gelu"))
        r_ps, r_max, r_exp, r_w = sem("r_ps"), sem("r_max"), sem("r_exp"), sem("r_w")
        gu_ps, gu_silu, moe_h, moe_hT_ps, moe_hT = (
            sem("gu_ps"), sem("gu_silu"), sem("moe_h"), sem("moe_hT_ps"), sem("moe_hT"))

        FIRST = [n for n, (name, _, _) in enumerate(CONST_INPUTS) if n <= 18 or name in ("kb1", "hm1")]
        REST = [n for n in range(len(CONST_INPUTS)) if n not in FIRST]

        class Attention:

            UNITS = TT * H // 2

            def __init__(self, tag, hd, masked):
                self.hd, self.masked = hd, masked
                self.tiles = 4 if hd == 16 else 8
                self.proj = sem(tag + "_proj")
                self.evac = sem(tag + "_evac")
                self.vevac = sem(tag + "_vevac")
                self.s_ps = sem(tag + "_s_ps")
                self.rmax = sem(tag + "_rmax")
                self.probs = sem(tag + "_probs")
                self.pT_ps = sem(tag + "_pT_ps")
                self.pT = sem(tag + "_pT")
                self.pv = sem(tag + "_pv")
                self.inv = sem(tag + "_inv")
                self.norm = sem(tag + "_norm")
                self.o = sem(tag + "_o")

            def score_bank(self, u):
                return (0, 1, 3)[u % 3]

            def queries(self, h):
                return QT[:, h % self.tiles, :]

            def keys(self, h):
                return KT16[:, h, :] if self.hd == 16 else KT64[h // 8][:, h % 8, :]

            def heads(self, u):
                return [u % (H // 2), u % (H // 2) + H // 2], u // (H // 2)

            def out_rows(self, u, j):
                if self.hd == 16:
                    start = 64 * (u % 2) + 32 * j
                    return slice(start, start + 32)
                return slice(64 * j, 64 * j + 64)

            def out_tile(self, u):
                hp = u % (H // 2)
                return hp // 2 if self.hd == 16 else hp

            def unit_rows(self, u):
                return slice(64 * (u % 2), 64 * (u % 2) + 64) if self.hd == 16 else slice(0, P)

        att0 = Attention("lat", 16, True)
        att1 = Attention("self", 16, False)
        att2 = Attention("cross", 64, False)

        block = ctx.enter_context(nc.Block())

        @block.sync
        def _(sp):
            sp.sem_inc(stored, 16)
            for n in FIRST:
                name, shape, _ = CONST_INPUTS[n]
                sp.dma_start(W[name][:], dram[name]).then_inc(w_first, 16)

            def load(i):
                sp.dma_start(x_in[:], dram["x"][i].rearrange("a p d -> p a d")).then_inc(loaded, 16)
                sp.dma_start(xT_in[:], dram["xT"][i].rearrange("a p d -> p a d")).then_inc(loaded, 16)

            def load_choices(i):
                sp.dma_start(idx[:], dram["idx"][i]).then_inc(idx_loaded, 16)

            def load_ctx(i):
                sp.dma_start(ctxT[:], dram["ctxT"][i].rearrange("a p d -> p a d")).then_inc(ctx_loaded, 16)

            def load_rows():
                for row, name in ((fb1, "fb1"), (ln2g, "ln2g"), (ln2b, "ln2b")):
                    sp.dma_start(row, dram[name]).then_inc(rows_loaded, 16)

            def store(i):
                sp.dma_start(out[i].rearrange("a p d -> p a d"), x_out).then_inc(stored, 16)

            load_choices(0)
            load(0)
            sp.dma_start(wst, dram["w1"]).then_inc(staged, 16)
            sp.dma_start(wst2, dram["w2"].rearrange("p a b -> p (a b)")).then_inc(staged, 16)
            load_ctx(0)
            for n in REST:
                name, shape, _ = CONST_INPUTS[n]
                sp.dma_start(W[name][:], dram[name]).then_inc(w_rest, 16)
            with sp.Fori(0, B - 1) as i:
                sp.wait_ge(sum_read, at(i, 6, 1))
                load_rows()
                load(i + 1)
                load_choices(i + 1)
                sp.wait_ge(att2.evac, at(i, 4, 4))
                sp.wait_ge(att2.vevac, at(i, 8, 8))
                load_ctx(i + 1)
                sp.wait_ge(batch_done, i + 2)
                store(i)
            sp.wait_ge(sum_read, at(B - 1, 6, 1))
            load_rows()
            load_choices(B - 1)
            sp.wait_ge(batch_done, B + 1)
            store(B - 1)
            sp.wait_ge(stored, 16 * (B + 1))

        @block.tensor
        def _(pe):
            mm, tr = nc.tensor.matmul, nc.tensor.transpose

            pe.wait_ge(setup_v, 2)
            pe.wait_ge(w_first, 16 * len(FIRST))
            mm(ps[:, 0, 0:2], W["ones"][:], wscale[:, 0:2], start=True, stop=True).then_inc(setup_t, 1)

            def x_transposed(i, version, nth):
                pe.wait_ge(x_ready, at(i, 5, version))
                for tt in range(TT):
                    for k in range(KD):
                        last = tr(ps[:, 7, k * T + tt * P:k * T + (tt + 1) * P],
                                  x[:, tt, k * P:(k + 1) * P], W["ident"][:])
                last.then_inc(xT_ps, 1)
                pe.wait_ge(xT_ready, at(i, 4, nth))

            def spread_b(i, u):
                if u >= 2:
                    pe.wait_ge(b_used, at(i, M * STEPS, u - 1))
                for n in range(NG):
                    s = u % STEPS * NG + n
                    last = mm(bank(u % 2 * 2 + n // 2)[:, n % 2, :],
                              W["sel"][:, s:s + 1].to_broadcast([96, P]), bcs[0:96, :],
                              start=True, stop=True)
                last.then_inc(b_ps, 1)

            def mamba(i):
                pe.wait_ge(loaded, at(i, 32, 32))
                for m in range(2 * M):
                    for k in range(KD):
                        last = mm(bank(4 + m // 2)[:, m % 2, :], W["win"][:, k, m * P:(m + 1) * P],
                                  xT_in[:, k, :], start=(k == 0), stop=(k == KD - 1))
                    if m % 2:
                        last.then_inc(xz, 1)
                for k in range(M):
                    pe.wait_ge(silu_x, at(i, M, k + 1))
                    mm(ps[0:RANK, 4, 0:T], W["wxd"][:, k, :], xc[:, k, :], start=(k == 0), stop=(k == M - 1))
                    last = mm(ps[0:96, 5, 0:T], W["wbc"][:, k, :], xc[:, k, :], start=(k == 0), stop=(k == M - 1))
                last.then_inc(xdbl, 1)
                pe.wait_ge(silu_z, at(i, 1, 1))
                pe.wait_ge(dtr_sb, at(i, 1, 1))
                for m in range(M):
                    last = mm(bank(6 + m // 2)[:, m % 2, :], W["wdt"][:, m * P:(m + 1) * P],
                              dtr[0:RANK, :], start=True, stop=True)
                    if m % 2:
                        last.then_inc(dt_ps, 1)

                def spread_c(n):
                    if n >= 4:
                        pe.wait_ge(c_sb, at(i, 8, n - 3))
                    for j in range(2):
                        s = NS + 2 * n + j
                        last = mm(bank(4 + n % 4)[:, j, :], W["sel"][:, s:s + 1].to_broadcast([96, P]),
                                  bcs[0:96, :], start=True, stop=True)
                    last.then_inc(c_ps, 1)

                pe.wait_ge(onehot, at(i, 1, 1))
                for q in range(P):
                    last = mm(ps[0:32, q // 32, (q % 32) * 16:(q % 32) * 16 + 16],
                              oh_hi[:, q, :], oh_lo[:, q, :], start=True, stop=True)
                    if q % 32 == 31:
                        last.then_inc(cnt_ps, 1)
                pe.wait_ge(bc_split, at(i, 1, 1))
                pe.wait_ge(cnt_sb, at(i, 4, 4))
                spread_c(0)
                psb = ps[:, 5, :].bitcast(BF16)
                for lo in range(16):
                    last = tr(psb[:, lo * 32:lo * 32 + 32], cnt[0:32, :, lo], W["identb"][0:32, 0:32])
                last.then_inc(cntT, 1)
                spread_b(i, 0)
                spread_b(i, 1)
                pe.wait_ge(cnt_max, at(i, 1, 1))
                pe.wait_ge(dt_x, at(i, 2, 2))
                for n in range(1, NS // 2):
                    spread_c(n)
                pe.wait_ge(c_sb, at(i, 8, 8))

                def sum_states(u):
                    m, g = u // STEPS, u % STEPS
                    pe.wait_ge(hc_ready, at(i, M * STEPS, u + 1))
                    if g == 0 and m >= 2:
                        pe.wait_ge(y_done, at(i, M, m - 1))
                    for n in range(NG):
                        last = mm(ps[:, 4 + m % 2, 0:T], W["ident"][:], hc[u % 2][:, n, :],
                                  start=(g == 0 and n == 0), stop=(g == STEPS - 1 and n == NG - 1))
                    last.then_inc(y_ready, 1)

                for u in range(M * STEPS):
                    if u + 2 < M * STEPS:
                        spread_b(i, u + 2)
                    sum_states(u)
                pe.wait_ge(y_done, at(i, M, M))
                for tt in range(TT):
                    for m in range(M):
                        last = mm(bank(6)[:, tt, :], yT[:, m, tt * P:(tt + 1) * P], W["wout"][:, m, :],
                                  start=(m == 0), stop=(m == M - 1))
                last.then_inc(sum_ps, 1)

            def attention(i, a, wo):
                hd = a.hd

                def scores(u):
                    hs, qt = a.heads(u)
                    if u >= 3:
                        pe.wait_ge(a.rmax if a.masked else a.probs, at(i, a.UNITS, u - 2))
                    for j, h in enumerate(hs):
                        last = mm(bank(a.score_bank(u))[:, j, :], a.queries(h)[:, qt * P:(qt + 1) * P], a.keys(h),
                                  start=True, stop=True)
                    last.then_inc(a.s_ps, 1)

                def turn(u):
                    pe.wait_ge(a.norm, at(i, a.UNITS, u + 1))
                    if u >= 2:
                        pe.wait_ge(a.pT, at(i, a.UNITS, u - 1))
                    for j in range(2):
                        for jt in range(TT):
                            last = tr(bank(4 + u % 2, 4)[:, 2 * j + jt, :],
                                      prob[u % 4][:, j, jt * P:(jt + 1) * P], W["ident"][:])
                    last.then_inc(a.pT_ps, 1)

                def times_v(u):
                    hs, qt = a.heads(u)
                    pe.wait_ge(a.pT, at(i, a.UNITS, u + 1))
                    if u >= 2:
                        pe.wait_ge(a.o, at(i, a.UNITS, u - 1))
                    for jt in range(TT):
                        for j, h in enumerate(hs):
                            w = VP[:, jt, h, :] if hd == 16 else VV[:, jt, h * hd:(h + 1) * hd]
                            last = mm(ps[a.out_rows(u, j), 6 + u % 2, 0:P], w, probT[u % 2][:, 2 * j + jt, :],
                                      start=(jt == 0), stop=(jt == TT - 1))
                    last.then_inc(a.pv, 1)

                def project(tt):
                    pe.wait_ge(a.o, at(i, a.UNITS, (tt + 1) * (H // 2)))
                    for k in range(a.tiles):
                        last = mm(bank(2)[:, tt, :], OT[:, k, tt * P:(tt + 1) * P], wo[:, k, :],
                                  start=(k == 0), stop=(k == a.tiles - 1))
                    return last

                for u in range(a.UNITS + 5):
                    if u < a.UNITS:
                        scores(u)
                    if 0 <= u - 3 < a.UNITS:
                        turn(u - 3)
                    if 0 <= u - 5:
                        times_v(u - 5)
                    if u == a.UNITS + 1:
                        project(0)
                project(1).then_inc(sum_ps, 1)

            def latent_projections(i):
                pe.wait_ge(w_rest, 16 * len(REST))
                pe.wait_ge(ctx_loaded, at(i, 16, 16))
                for k in range(KD):
                    last = mm(ps[:, 5, 0:T], W["wdown0"][:, k, :], ctxT[:, k, :], start=(k == 0), stop=(k == KD - 1))
                last.then_inc(att0.proj, 1)
                for t in range(4):
                    for k in range(KD):
                        last = mm(bank(t // 2)[:, t % 2, :], W["wq0"][:, k, t * P:(t + 1) * P], xT[:, k, :],
                                  start=(k == 0), stop=(k == KD - 1))
                last.then_inc(att0.proj, 1)
                pe.wait_ge(att0.evac, at(i, 3, 1))
                for t in range(4):
                    last = mm(bank(2 + t // 2)[:, t % 2, :], W["wk0"][:, t * P:(t + 1) * P], ckvT,
                              start=True, stop=True)
                last.then_inc(att0.proj, 1)
                for tt in range(TT):
                    last = mm(bank(4)[:, tt, :], ckvT[:, tt * P:(tt + 1) * P], W["wv0"][:], start=True, stop=True)
                last.then_inc(att0.proj, 1)
                pe.wait_ge(att0.evac, at(i, 3, 3))
                pe.wait_ge(att0.vevac, at(i, 1, 1))

            def self_projections(i):
                for first, w in ((0, W["wq1"]), (2, W["wk1"])):
                    for t in range(4):
                        for k in range(KD):
                            last = mm(bank(first + t // 2)[:, t % 2, :], w[:, k, t * P:(t + 1) * P], xT[:, k, :],
                                      start=(k == 0), stop=(k == KD - 1))
                    last.then_inc(att1.proj, 1)
                for tt in range(TT):
                    for k in range(KD):
                        last = mm(bank(4)[:, tt, :], xT[:, k, tt * P:(tt + 1) * P], W["wv1"][:, k, :],
                                  start=(k == 0), stop=(k == KD - 1))
                last.then_inc(att1.proj, 1)
                pe.wait_ge(att1.evac, at(i, 1, 1))
                pe.wait_ge(att1.vevac, at(i, 2, 2))

            def cross_projections(i):
                for n, b in enumerate((0, 1, 2, 7)):
                    for t in (2 * n, 2 * n + 1):
                        for k in range(KD):
                            last = mm(bank(b)[:, t % 2, :], W["wq2"][:, k, t * P:(t + 1) * P], xT[:, k, :],
                                      start=(k == 0), stop=(k == KD - 1))
                    last.then_inc(att2.proj, 1)
                for n in range(4):
                    for t in (2 * n, 2 * n + 1):
                        for k in range(KD):
                            last = mm(bank(3 + n)[:, t % 2, :], W["wk2"][:, k, t * P:(t + 1) * P], ctxT[:, k, :],
                                      start=(k == 0), stop=(k == KD - 1))
                    last.then_inc(att2.proj, 1)
                for n in range(4):
                    b = (0, 1, 2, 7)[n]
                    pe.wait_ge(att2.vevac, at(i, 8, n + 1))
                    for k in range(KD):
                        last = mm(ps[:, b, :], ctxT[:, k, n // 2 * P:(n // 2 + 1) * P],
                                  W["wv2"][:, k, n % 2 * 512:(n % 2 + 1) * 512],
                                  start=(k == 0), stop=(k == KD - 1))
                    last.then_inc(att2.proj, 1)
                pe.wait_ge(att2.evac, at(i, 4, 4))
                pe.wait_ge(att2.vevac, at(i, 8, 8))

            def ffn(i):
                psb = ps[:, 6, :].bitcast(BF16).rearrange("p (a b) -> p a b", b=T)
                pe.wait_ge(f_q, at(i, 2, 1))
                for tt in range(TT):
                    for k in range(KD):
                        last = tr(psb[:, k, tt * P:(tt + 1) * P], qb[:, tt, k * P:(k + 1) * P], W["identb"][:])
                last.then_inc(f_qT_ps, 1)
                pe.wait_ge(f_qT, at(i, 3, 1))
                for tt in range(TT):
                    for half in range(2):
                        for k in range(KD):
                            last = mm(ps[:, 2 * tt + half, :], qT[:, k, tt * P:(tt + 1) * P],
                                      w1q[:, k, half * 512:(half + 1) * 512], start=(k == 0), stop=(k == KD - 1))
                    last.then_inc(f_h_ps, 1)
                pe.wait_ge(f_q, at(i, 2, 2))
                for n in range(2):
                    psb = ps[:, 4 + n, :].bitcast(BF16).rearrange("p (a b) -> p a b", b=T)
                    for k in range(4):
                        for tt in range(TT):
                            last = tr(psb[:, k, tt * P:(tt + 1) * P],
                                      qb[:, tt, (4 * n + k) * P:(4 * n + k + 1) * P], W["identb"][:])
                    last.then_inc(f_qT_ps, 1)
                pe.wait_ge(f_qT, at(i, 3, 3))
                for tt in range(TT):
                    for k in range(KF):
                        last = mm(bank(6)[:, tt, :], qT[:, k, tt * P:(tt + 1) * P], w2q[:, k, :],
                                  start=(k == 0), stop=(k == KF - 1))
                last.then_inc(sum_ps, 1)

            def moe(i):
                for tt in range(TT):
                    for k in range(KD):
                        last = mm(ps[:, 6, tt * E:(tt + 1) * E], xT[:, k, tt * P:(tt + 1) * P], W["router"][:, k, :],
                                  start=(k == 0), stop=(k == KD - 1))
                last.then_inc(r_ps, 1)

                def gate_up(c):
                    tt, lo, n = c // 3, c % 3 * 512, min(512, MOE - c % 3 * 512)
                    if c >= 3:
                        pe.wait_ge(moe_h, at(i, 6, c - 2))
                    for b, w in ((0, W["wgate"]), (1, W["wup"])):
                        for k in range(KD):
                            last = mm(ps[:, c % 3 * 2 + b, 0:n], xT[:, k, tt * P:(tt + 1) * P], w[:, k, lo:lo + n],
                                      start=(k == 0), stop=(k == KD - 1))
                    last.then_inc(gu_ps, 1)

                def turn(c):
                    tt, k0, n = c // 3, c % 3 * 4, min(4, KM - c % 3 * 4)
                    pe.wait_ge(moe_h, at(i, 6, c + 1))
                    if c >= 2:
                        pe.wait_ge(moe_hT, at(i, 6, c - 1))
                    for k in range(n):
                        last = tr(bank(6 + c % 2, 4)[:, k, :], mh[:, tt, (k0 + k) * P:(k0 + k + 1) * P], W["ident"][:])
                    last.then_inc(moe_hT_ps, 1)

                for c in range(8):
                    if c < 6:
                        gate_up(c)
                    if c >= 2:
                        turn(c - 2)
                pe.wait_ge(moe_hT, at(i, 6, 6))
                for tt in range(TT):
                    for k in range(KM):
                        last = mm(bank(0)[:, tt, :], mhT[:, k, tt * P:(tt + 1) * P], W["wmoe"][:, k, :],
                                  start=(k == 0), stop=(k == KM - 1))
                last.then_inc(sum_ps, 1)

            with pe.Fori(0, B) as i:
                mamba(i)
                x_transposed(i, 1, 1)
                latent_projections(i)
                attention(i, att0, W["wo0"])
                ffn(i)
                x_transposed(i, 3, 2)
                self_projections(i)
                attention(i, att1, W["wo1"])
                x_transposed(i, 4, 3)
                cross_projections(i)
                attention(i, att2, W["wo2"])
                x_transposed(i, 5, 4)
                moe(i)

        @block.scalar
        def _(act):
            f = nc.scalar.activation

            act.wait_ge(w_first, 16 * len(FIRST))
            act.preload_act_table_set(EXP_LN)
            f(aneg[:], W["alog"][:], ACT.Exp).then_inc(setup_a, 1)
            act.wait_ge(setup_v, 1)

            def rstd_guess_of(i, c, n):
                act.wait_ge(var_ready, at(i, 8, n))
                c.link(f(lnv[:], mv[:, :, 1], ACT.Ln, bias=epsc[:, 0:1]))
                f(rstd[:], lnv[:], ACT.Exp, scale=-0.5).then_inc(rstd_guess, 1)

            def xT_copy(i, nth):
                act.wait_ge(xT_ps, at(i, 4, nth))
                f(xT[:], bank(7), ACT.Copy).then_inc(xT_ready, 1)

            def mamba(i, c):
                for b in range(2):
                    act.wait_ge(xz, at(i, 4, b + 1))
                    f(xin[:, 2 * b:2 * b + 2, TAPS - 1:], bank(4 + b), ACT.Copy).then_inc(xin_sb, 1)
                act.preload_act_table_set(SILU_SET)
                for m in range(M):
                    act.wait_ge(conv_done, at(i, M, m + 1))
                    f(xc[:, m, :], conv[:, m, :], ACT.Silu).then_inc(silu_x, 1)
                act.wait_ge(xz, at(i, 4, 4))
                f(zs, ps[:, 6:8, :].rearrange("p a b -> p (a b)").rearrange("p (m t) -> p m t", t=T),
                  ACT.Silu).then_inc(silu_z, 1)
                act.preload_act_table_set(EXP_LN)
                act.wait_ge(xdbl, at(i, 1, 1))
                f(dtr[0:RANK, :], ps[0:RANK, 4, 0:T], ACT.Copy).then_inc(dtr_sb, 1)
                for half in range(2):
                    ms = slice(2 * half, 2 * half + 2)
                    act.wait_ge(dt_x, at(i, 2, half + 1))
                    c.link(f(sp_e[:, ms], sp_x[:, ms], ACT.Abs))
                    c.link(f(sp_e[:, ms], sp_e[:, ms], ACT.Exp, scale=-1.0))
                    f(sp_l[:, ms], sp_e[:, ms], ACT.Ln, bias=onec[:, 0:1]).then_inc(dt_ln, 1)
                for n in range(4):
                    act.wait_ge(cnt_ps, at(i, 4, n + 1))
                    f(cnt[0:32, 32 * n:32 * n + 32, :],
                      ps[0:32, n, :].rearrange("p (q l) -> p q l", l=16), ACT.Copy).then_inc(cnt_sb, 1)
                act.wait_ge(dt_done, at(i, 2, 1))
                act.wait_ge(pads, at(i, 2, 2))

                def decays(u):
                    m, g = u // STEPS, u % STEPS
                    if u >= 2:
                        act.wait_ge(h_ready, at(i, M * STEPS, u - 1))
                    for n in range(NG):
                        s = g * NG + n
                        last = f(decay[u % 2][:, n, 1:T], dt[:, m, 1:T], ACT.Exp, scale=aneg[:, m, s:s + 1])
                    last.then_inc(decay_ready, 1)

                decays(0)
                act.wait_ge(cnt_max, at(i, 1, 1))
                f(cm1, cm1, ACT.Ln).then_inc(cnt_ln, 1)
                decays(1)
                act.wait_ge(dt_done, at(i, 2, 2))
                for n in range(8):
                    act.wait_ge(c_ps, at(i, 8, n + 1))
                    f(csb[:, 2 * n:2 * n + 2, :], bank(4 + n % 4), ACT.Copy).then_inc(c_sb, 1)
                for u in range(2, M * STEPS):
                    decays(u)

            def attention(i, c, a):
                def output(u):
                    act.wait_ge(a.pv, at(i, a.UNITS, u + 1))
                    r, qt = a.unit_rows(u), u // (H // 2)
                    f(OT[r, a.out_tile(u), qt * P:(qt + 1) * P], ps[r, 6 + u % 2, 0:P], ACT.Copy).then_inc(a.o, 1)

                for u in range(a.UNITS):
                    if u >= 6:
                        output(u - 6)
                    act.wait_ge(a.rmax, at(i, a.UNITS, u + 1))
                    if u >= 4:
                        act.wait_ge(a.pT_ps, at(i, a.UNITS, u - 3))
                    for j in range(2):
                        src = smask[u % 2][:, j, :] if a.masked else bank(a.score_bank(u))[:, j, :]
                        last = f(prob[u % 4][:, j, :], src, ACT.Exp, bias=rmax[:, 2 * u + j:2 * u + j + 1],
                                 scale=-1.0 if a.masked else 1.0, accum_out=rsum[:, 2 * u + j:2 * u + j + 1])
                    last.then_inc(a.probs, 1)
                for u in range(a.UNITS - 6, a.UNITS):
                    output(u)

            with act.Fori(0, B) as i:
                c = Chain(act, a_step, i, A_STEPS)
                mamba(i, c)
                rstd_guess_of(i, c, 1)
                xT_copy(i, 1)
                act.wait_ge(att0.proj, at(i, 4, 1))
                f(ckvT, ps[:, 5, 0:T], ACT.Copy).then_inc(att0.evac, 1)
                act.wait_ge(att0.proj, at(i, 4, 2))
                f(QT[:, 0:4, :], ps[:, 0:2, :].rearrange("p a (b t) -> p (a b) t", t=T), ACT.Copy,
                  scale=0.25).then_inc(att0.evac, 1)
                act.wait_ge(att0.proj, at(i, 4, 3))
                for g in range(4):
                    last = f(KT16[:, 4 * g:4 * g + 2, :], bank(2),
                             ACT.Copy, scale=W["group"][:, g:g + 1])
                last.then_inc(att0.evac, 1)
                attention(i, c, att0)
                rstd_guess_of(i, c, 2)
                rstd_guess_of(i, c, 3)
                act.wait_ge(f_qT_ps, at(i, 3, 1))
                f(qT[:, 0:KD, :], ps[:, 6, :].bitcast(BF16).rearrange("p (k t) -> p k t", t=T)[:, 0:KD, :],
                  ACT.Copy).then_inc(f_qT, 1)
                act.preload_act_table_set(GELU_SET)
                for tt in range(TT):
                    act.wait_ge(f_h, at(i, TT, tt + 1))
                    f(fh[:, tt, :], fh[:, tt, :], ACT.Gelu).then_inc(f_gelu, 1)
                act.preload_act_table_set(EXP_LN)
                rstd_guess_of(i, c, 4)
                for n in range(2):
                    act.wait_ge(f_qT_ps, at(i, 3, n + 2))
                    f(qT[:, 4 * n:4 * n + 4, :], ps[:, 4 + n, :].bitcast(BF16).rearrange("p (k t) -> p k t", t=T),
                      ACT.Copy).then_inc(f_qT, 1)
                rstd_guess_of(i, c, 5)
                xT_copy(i, 2)
                act.wait_ge(att1.proj, at(i, 3, 2))
                for g in range(4):
                    for t in range(2):
                        last = f(KT16[:, 4 * g + t, :], bank(2)[:, t, :], ACT.Identity,
                                 bias=kbh[:, g, t:t + 1], scale=hmk[:, g, t:t + 1])
                last.then_inc(att1.evac, 1)
                attention(i, c, att1)
                rstd_guess_of(i, c, 6)
                xT_copy(i, 3)
                for n in range(4):
                    act.wait_ge(att2.proj, at(i, 12, 5 + n))
                    for side in range(2):
                        last = f(KT64[side][:, 2 * n:2 * n + 2, :], bank(3 + n), ACT.Copy, scale=W["side"][:, side:side + 1])
                    last.then_inc(att2.evac, 1)
                attention(i, c, att2)
                rstd_guess_of(i, c, 7)
                xT_copy(i, 4)
                for tt in range(TT):
                    act.wait_ge(r_max, at(i, 1, 1))
                    last = f(route[:, 0, tt, :], ps[:, 6, tt * E:(tt + 1) * E], ACT.Exp, bias=rs2[:, 0, tt:tt + 1])
                last.then_inc(r_exp, 1)
                act.preload_act_table_set(SILU_SET)

                def moe_turned(k):
                    tt, k0, n = k // 3, k % 3 * 4, min(4, KM - k % 3 * 4)
                    act.wait_ge(moe_hT_ps, at(i, 6, k + 1))
                    f(mhT[:, k0:k0 + n, tt * P:(tt + 1) * P], bank(6 + k % 2, 4)[:, 0:n, :],
                      ACT.Copy).then_inc(moe_hT, 1)

                for k in range(8):
                    if k < 6:
                        tt, lo, n = k // 3, k % 3 * 512, min(512, MOE - k % 3 * 512)
                        act.wait_ge(gu_ps, at(i, 6, k + 1))
                        f(sg[:, tt, lo:lo + n], ps[:, k % 3 * 2, 0:n], ACT.Silu).then_inc(gu_silu, 1)
                    if k >= 2:
                        moe_turned(k - 2)
                act.preload_act_table_set(EXP_LN)
                rstd_guess_of(i, c, 8)
                c.close()

        @block.gpsimd
        def _(pool):
            with pool.Fori(0, B) as i:
                pool.wait_ge(c_sb, at(i, 8, 8))
                pool.wait_ge(stored, at(i, 16, 16))
                for u in range(M * STEPS):
                    pool.wait_ge(h_ready, at(i, M * STEPS, u + 1))
                    if u >= 2:
                        pool.wait_ge(y_ready, at(i, M * STEPS, u - 1))
                    g = u % STEPS
                    nc.gpsimd.tensor_tensor(hc[u % 2], hbuf[u % 2], csb[:, g * NG:(g + 1) * NG, :],
                                            ALU.mult).then_inc(hc_ready, 1)
                for a in (att0, att1, att2):
                    for u in range(a.UNITS):
                        pool.wait_ge(a.inv, at(i, a.UNITS, u + 1))
                        nc.gpsimd.tensor_tensor(prob[u % 4], prob[u % 4],
                                                rinv[:, 2 * u:2 * u + 2].unsqueeze(2).to_broadcast([P, 2, T]),
                                                ALU.mult).then_inc(a.norm, 1)

        @block.vector
        def _(v):
            tt_, ts, stt, cp = nc.vector.tensor_tensor, nc.vector.tensor_scalar, nc.vector.scalar_tensor_tensor, nc.vector.tensor_copy

            nc.vector.memset(epsc[:], EPS).then_inc(setup_v, 1)
            v.wait_ge(staged, 32)
            nc.vector.tensor_reduce(wscale[:, 0:1], wst.rearrange("p a b -> p (a b)"), AX, ALU.add,
                                    apply_absolute_value=True)
            nc.vector.tensor_reduce(wscale[:, 1:2], wst2.rearrange("p a b -> p (a b)"), AX, ALU.add,
                                    apply_absolute_value=True).then_inc(setup_v, 1)
            v.wait_ge(setup_a, 1)
            ts(aneg[:], aneg[:], -1.0, None, ALU.mult).then_inc(setup_v, 1)
            v.wait_ge(setup_t, 1)
            ts(wscale[:, 2:4], ps[:, 0, 0:2], 1.0 / (D * FF), 1e-5, ALU.mult, ALU.max).then_inc(setup_v, 1)
            v.wait_ge(setup_v, 4)
            nc.vector.reciprocal(wscale[:, 4:6], wscale[:, 2:4]).then_inc(setup_v, 1)
            v.wait_ge(setup_v, 5)
            n = 5
            flat = [(wst, wscale[:, 4:5], w1q[:].rearrange("p a b -> p (a b)")),
                    (wst2, wscale[:, 5:6], w2q[:].rearrange("p a b -> p (a b)"))]
            for w, inv, q in flat:
                w = w.rearrange("p a b -> p (a b)")
                for o, s1, s2, op0, op1 in ((w, inv, ROUND, ALU.mult, ALU.add),
                                            (w, -ROUND, -1.0, ALU.add, ALU.max),
                                            (q, 1.0, None, ALU.min, ALU.bypass)):
                    ts(o, w, s1, s2, op0, op1).then_inc(setup_v, 1)
                    n += 1
                    v.wait_ge(setup_v, n)
            for g in range(4):
                ts(hmk[:, g, :], W["hm1"][:], W["group"][:, g:g + 1], None, ALU.mult).then_inc(setup_v, 1)
            ts(hmq[:], W["hm1"][:], 0.25, None, ALU.mult).then_inc(setup_v, 1)
            v.wait_ge(setup_v, n + 5)
            for g in range(4):
                tt_(kbh[:, g, :], W["kb1"][:], hmk[:, g, :], ALU.mult).then_inc(setup_v, 1)
            v.wait_ge(setup_v, n + 9)
            nc.vector.memset(onec[:], 1.0).then_inc(batch_done, 1)

            def normalised(i, c, n, src, dst, width, gain=None, bias=None):
                parts = max(1, width // 512)
                for tt in range(TT):
                    for p in range(parts):
                        w = width // parts
                        c.did(nc.vector.bn_stats(stats[:, tt, p, :], src[:, tt, p * w:(p + 1) * w]))
                c.settle()
                nc.vector.memset(spare[:, n:n + 1], 0.0)
                for tt in range(TT):
                    last = nc.vector.bn_aggr(mv[:, tt, :], stats[:, tt, 0:parts, :].rearrange("p a b -> p (a b)"))
                last.then_inc(var_ready, 1)
                if gain is not None:
                    v.wait_ge(var_ready, at(i, 8, n))
                    for tt in range(TT):
                        c.did(stt(dst[:, tt, :], src[:, tt, :], mv[:, tt, 0:1], gain, ALU.subtract, ALU.mult))
                v.wait_ge(rstd_guess, at(i, 8, n))
                c.link(stt(nt[:], mv[:, :, 1], EPS, rstd[:], ALU.add, ALU.mult))
                c.link(stt(nt[:], nt[:], -0.5, rstd[:], ALU.mult, ALU.mult))
                c.link(stt(rstd[:], nt[:], 1.5, rstd[:], ALU.add, ALU.mult))
                for tt in range(TT):
                    if gain is None:
                        last = ts(dst[:, tt, :], src[:, tt, :], mv[:, tt, 0:1], rstd[:, tt:tt + 1],
                                  ALU.subtract, ALU.mult)
                    else:
                        last = stt(dst[:, tt, :], dst[:, tt, :], rstd[:, tt:tt + 1], bias, ALU.mult, ALU.add)
                return last

            def residual(i, c, n, b, addend, dst, done, dequant=None):
                v.wait_ge(sum_ps, at(i, 6, n))
                tt_(res, bank(b), addend, ALU.add).then_inc(sum_read, 1)
                v.wait_ge(sum_read, at(i, 6, n))
                return res

            def quantised(i, c, src, width, wcol):
                c.link(nc.vector.tensor_reduce(small[:, 0, :], src, AX, ALU.max, apply_absolute_value=True))
                c.link(ts(small[:, 1, :], small[:, 0, :], 1e-5, None, ALU.max))
                c.did(nc.vector.reciprocal(small[:, 2, :], small[:, 1, :]))
                c.did(ts(small[:, 4, :], small[:, 1, :], 1.0 / 127.0, wscale[:, wcol:wcol + 1], ALU.mult, ALU.mult))
                c.settle()
                c.link(ts(small[:, 3, :], small[:, 2, :], 127.0, None, ALU.mult))
                for tt in range(TT):
                    c.did(ts(src[:, tt, :], src[:, tt, :], small[:, 3, tt:tt + 1], -128.0, ALU.mult, ALU.max))
                c.settle()
                c.did(ts(src, src, 127.0, ROUND, ALU.min, ALU.add))
                c.settle()
                return ts(qb[:, :, 0:width], src, -ROUND, None, ALU.add)

            def digits(c):
                c.link(cp(ix[0], idx[:]))
                c.link(ts(ix[1], ix[0], 0.0, float(T), ALU.is_lt, ALU.mult))
                c.link(tt_(ix[2], ix[0], ix[1], ALU.add))
                c.link(ts(ixi[3], ix[2], 0.0, float(T - 1), ALU.max, ALU.min))
                c.did(ts(ixi[4], ixi[3], 4, None, ALU.logical_shift_right))
                c.did(ts(ixi[5], ixi[3], 15, None, ALU.bitwise_and))
                c.settle()
                c.did(ts(hib, ixi[4], W["half"][:, 0:1], None, ALU.add))
                c.link(cp(lob, ixi[5]))

            def one_hots(lo, n):
                for o, digit, width in ((oh_hi, hib, 32), (oh_lo, lob, 16)):
                    last = tt_(o[:, lo:lo + n, :], digit[:, lo:lo + n].unsqueeze(2).to_broadcast([P, n, width]),
                               W["iota"][:, 0:width].unsqueeze(1).to_broadcast([P, n, width]), ALU.is_equal)
                return last

            def mamba(i, c):
                v.wait_ge(batch_done, i + 1)
                v.wait_ge(loaded, at(i, 32, 32))
                c.link(nc.vector.memset(xin[:, :, 0:TAPS - 1], 0.0))
                for half in range(2):
                    v.wait_ge(xin_sb, at(i, 2, half + 1))
                    for m in (2 * half, 2 * half + 1):
                        c.did(ts(conv[:, m, :], xin[:, m, 0:T], W["convw"][:, m, 0:1], W["convb"][:, m:m + 1],
                                 ALU.mult, ALU.add))
                    for k in range(1, TAPS):
                        c.settle()
                        for m in (2 * half, 2 * half + 1):
                            ins = stt(conv[:, m, :], xin[:, m, k:k + T], W["convw"][:, m, k:k + 1], conv[:, m, :],
                                      ALU.mult, ALU.add)
                            if k < TAPS - 1:
                                c.did(ins)
                            else:
                                ins.then_inc(conv_done, 1)
                v.wait_ge(xdbl, at(i, 1, 1))
                c.link(cp(bcs[0:96, :], ps[0:96, 5, 0:T]))
                c.link(tt_(br1[0:96, :], ps[0:96, 5, 0:T], bcs[0:96, :], ALU.subtract))
                c.link(cp(bmid[0:96, :], br1[0:96, :]))
                cp(bcs[32:64, :], bmid[32:64, :])
                tt_(bcs[64:96, :], br1[64:96, :], bmid[64:96, :], ALU.subtract).then_inc(bc_split, 1)
                for half in range(2):
                    v.wait_ge(dt_ps, at(i, 2, half + 1))
                    for m in (2 * half, 2 * half + 1):
                        last = ts(sp_x[:, m, :], bank(6 + half)[:, m % 2, :], W["bdt"][:, m:m + 1], None, ALU.add)
                    last.then_inc(dt_x, 1)
                for half in range(2):
                    ms = slice(2 * half, 2 * half + 2)
                    v.wait_ge(dt_ln, at(i, 2, half + 1))
                    c.link(ts(dt[:, ms], sp_e[:, ms], 1.0, None, ALU.add))
                    c.did(stt(dtx[:, ms], dt[:, ms], 1.0, sp_e[:, ms], ALU.subtract, ALU.subtract))
                    c.did(stt(sp_x[:, ms], sp_x[:, ms], 0.0, sp_l[:, ms], ALU.max, ALU.add))
                    c.settle()
                    tt_(dt[:, ms], sp_x[:, ms], dtx[:, ms], ALU.subtract).then_inc(dt_done, 1)
                v.wait_ge(cntT, at(i, 1, 1))
                for s in range(2):
                    nc.vector.memset(decay[s][:, :, 0:1], 0.0).then_inc(pads, 1)
                counts = ps[:, 5, 0:256].bitcast(BF16).rearrange("q (l t h) -> q t h l", l=16, t=TT)
                as4 = lambda ap: ap.rearrange("q t (h l) -> q t h l", l=16)
                for t in range(TT):
                    ts(as4(cm1)[:, t], counts[:, t], 1.0, None, ALU.max)
                    last = ts(as4(cm0)[:, t], counts[:, t], 0.0, MASKED, ALU.is_equal, ALU.mult)
                last.then_inc(cnt_max, 1)
                v.wait_ge(dt_done, at(i, 2, 2))
                c.link(tt_(dtx, dt, xc, ALU.mult))

                def gate(m):
                    v.wait_ge(y_ready, at(i, M * STEPS, STEPS * (m + 1)))
                    c.link(stt(yT[:, m, :], xc[:, m, :], W["dp"][:, m:m + 1], ps[:, 4 + m % 2, 0:T], ALU.mult, ALU.add))
                    tt_(yT[:, m, :], yT[:, m, :], zs[:, m, :], ALU.mult).then_inc(y_done, 1)

                for u in range(M * STEPS):
                    m = u // STEPS
                    v.wait_ge(b_ps, at(i, M * STEPS, u + 1))
                    if u >= 2:
                        v.wait_ge(hc_ready, at(i, M * STEPS, u - 1))
                    b = ps[:, u % 2 * 2:u % 2 * 2 + 2, :].rearrange("p a (b t) -> p (a b) t", t=T)
                    tt_(hbuf[u % 2], dtx[:, m, :].unsqueeze(1).to_broadcast([P, NG, T]), b, ALU.mult).then_inc(b_used, 1)
                    if u == 0:
                        v.wait_ge(cnt_ln, at(i, 1, 1))
                        c.did(tt_(mask[:], cm1, cm0, ALU.add))
                    v.wait_ge(b_used, at(i, M * STEPS, u + 1))
                    v.wait_ge(decay_ready, at(i, M * STEPS, u + 1))
                    flat = lambda ap: ap.rearrange("p a b -> p (a b)")
                    nc.vector.tensor_tensor_scan(flat(hbuf[u % 2]), flat(decay[u % 2]), flat(hbuf[u % 2]), 0.0,
                                                 ALU.mult, ALU.add).then_inc(h_ready, 1)
                    if u % STEPS == 2 and m >= 1:
                        gate(m - 1)
                gate(M - 1)

            def attention(i, c, a):
                for u in range(a.UNITS + 4):
                    if u < a.UNITS:
                        qt = u // (H // 2)
                        v.wait_ge(a.s_ps, at(i, a.UNITS, u + 1))
                        if a.masked:
                            if u >= 2:
                                v.wait_ge(a.probs, at(i, a.UNITS, u - 1))
                            nc.vector.memset(spare[:, 9 + u:10 + u], 0.0)
                            for j in range(2):
                                last = nc.vector.tensor_tensor_reduce(
                                    smask[u % 2][:, j, :], bank(a.score_bank(u))[:, j, :], mask[:, qt, :], -1.0, HUGE,
                                    ALU.add, ALU.min, rmax[:, 2 * u + j:2 * u + j + 1])
                        else:
                            last = nc.vector.tensor_reduce(rmax[:, 2 * u:2 * u + 2], bank(a.score_bank(u)), AX, ALU.max,
                                                           negate=True)
                        last.then_inc(a.rmax, 1)
                    if 0 <= u - 1 < a.UNITS:
                        w = u - 1
                        v.wait_ge(a.probs, at(i, a.UNITS, w + 1))
                        nc.vector.reciprocal(rinv[:, 2 * w:2 * w + 2], rsum[:, 2 * w:2 * w + 2]).then_inc(a.inv, 1)
                    if 0 <= u - 4:
                        w = u - 4
                        v.wait_ge(a.pT_ps, at(i, a.UNITS, w + 1))
                        if w >= 2:
                            v.wait_ge(a.pv, at(i, a.UNITS, w - 1))
                        cp(probT[w % 2], bank(4 + w % 2, 4)).then_inc(a.pT, 1)

            def ffn(i, c):
                hn = fq[:, :, 0:D]
                c.link(normalised(i, c, 3, x[:], hn, D, W["ln1g"][:], W["ln1b"][:]))
                quantised(i, c, hn, D, 2).then_inc(f_q, 1)
                v.wait_ge(rows_loaded, at(i, 48, 48))
                for tt in range(TT):
                    v.wait_ge(f_h_ps, at(i, TT, tt + 1))
                    stt(fh[:, tt, :], ps[:, 2 * tt:2 * tt + 2, :].rearrange("p a b -> p (a b)"),
                        small[:, 4, tt:tt + 1], fb1, ALU.mult, ALU.add).then_inc(f_h, 1)
                v.wait_ge(f_gelu, at(i, TT, 2))
                c.link(normalised(i, c, 4, fh, fq, FF, ln2g, ln2b))
                quantised(i, c, fq, FF, 3).then_inc(f_q, 1)
                c.link(tt_(x[:], x[:], W["fb2"][:].unsqueeze(1).to_broadcast([P, TT, D]), ALU.add))
                v.wait_ge(sum_ps, at(i, 6, 3))
                for tt in range(TT):
                    last = stt(res[:, tt, :], bank(6)[:, tt, :], small[:, 4, tt:tt + 1], x[:, tt, :], ALU.mult, ALU.add)
                last.then_inc(sum_read, 1)
                v.wait_ge(sum_read, at(i, 6, 3))

            def moe(i, c):
                v.wait_ge(r_ps, at(i, 1, 1))
                logits = ps[:, 6, 0:TT * E].rearrange("p (t e) -> p t e", e=E)
                nc.vector.tensor_reduce(rs2[:, 0, :], logits, AX, ALU.max, negate=True).then_inc(r_max, 1)
                v.wait_ge(r_exp, at(i, 1, 1))
                c.link(nc.vector.tensor_reduce(rs2[:, 1, :], route[:, 0], AX, ALU.add))
                c.link(nc.vector.reciprocal(rs2[:, 2, :], rs2[:, 1, :]))
                c.link(tt_(route[:, 1], route[:, 0], rs2[:, 2, :].unsqueeze(2).to_broadcast([P, TT, E]), ALU.mult))
                for tt in range(TT):
                    mine = route[:, 1, tt, :].unsqueeze(2).to_broadcast([P, E, E])
                    other = route[:, 1, tt, :].unsqueeze(1).to_broadcast([P, E, E])
                    c.did(tt_(rcmp[:, 0, tt], other, mine, ALU.is_gt))
                    c.did(tt_(rcmp[:, 1, tt], other, mine, ALU.is_equal))
                c.settle()
                for tt in range(TT):
                    c.did(tt_(rcmp[:, 1, tt], rcmp[:, 1, tt], W["tri"][:], ALU.mult))
                c.settle()
                c.link(tt_(rcmp[:, 0].rearrange("p t a b -> p (t a b)"), rcmp[:, 0].rearrange("p t a b -> p (t a b)"),
                           rcmp[:, 1].rearrange("p t a b -> p (t a b)"), ALU.add))
                c.link(nc.vector.tensor_reduce(route[:, 2].rearrange("p t e -> p (t e)"),
                                               rcmp[:, 0].rearrange("p t a b -> p (t a) b"), AX, ALU.add))
                c.link(stt(route[:, 3], route[:, 2], float(TOPK), route[:, 1], ALU.is_lt, ALU.mult))
                for k in range(6):
                    tt, lo, n = k // 3, k % 3 * 512, min(512, MOE - k % 3 * 512)
                    v.wait_ge(gu_silu, at(i, 6, k + 1))
                    up = ps[:, k % 3 * 2 + 1, 0:n]
                    if n == 512:
                        for e in range(4):
                            w = route[:, 3, tt, lo // FE + e:lo // FE + e + 1]
                            last = stt(mh[:, tt, lo + e * FE:lo + (e + 1) * FE], sg[:, tt, lo + e * FE:lo + (e + 1) * FE], w,
                                       up[:, e * FE:(e + 1) * FE], ALU.mult, ALU.mult)
                    else:
                        last = tt_(mh[:, tt, lo:lo + n], sg[:, tt, lo:lo + n], up, ALU.mult)
                    last.then_inc(moe_h, 1)
                    if k == 0:
                        v.wait_ge(idx_loaded, at(i, 16, 32))
                        digits(c)
                    elif k < 5:
                        last = one_hots((k - 1) * 32, 32)
                        if k == 4:
                            last.then_inc(onehot, 1)

            v.wait_ge(w_first, 16 * len(FIRST))
            v.wait_ge(idx_loaded, 16)
            c = Chain(v, choices_step, 0, CHOICES_STEPS)
            digits(c)
            c.close()
            one_hots(0, P).then_inc(onehot, 1)

            with v.Fori(0, B) as i:
                c = Chain(v, v_step, i, V_STEPS)
                bc = lambda w: w.unsqueeze(1).to_broadcast([P, TT, D])
                mamba(i, c)
                residual(i, c, 1, 6, x_in[:], None, None)
                normalised(i, c, 1, res, x, D).then_inc(x_ready, 1)
                v.wait_ge(att0.proj, at(i, 4, 3))
                for g in range(4):
                    ts(KT16[:, 4 * g + 2:4 * g + 4, :], bank(3), W["group"][:, g:g + 1], None, ALU.mult)
                v.wait_ge(att0.proj, at(i, 4, 4))
                nc.vector.memset(VP[:, :, :, 16:32], 0.0)
                cp(VP[:, :, :, 0:16], bank(4).rearrange("p t (h d) -> p t h d", d=16)).then_inc(att0.vevac, 1)
                attention(i, c, att0)
                residual(i, c, 2, 2, x[:], None, None)
                normalised(i, c, 2, res, x, D).then_inc(x_ready, 1)
                v.wait_ge(x_ready, at(i, 5, 2))
                ffn(i, c)
                normalised(i, c, 5, res, x, D).then_inc(x_ready, 1)
                for t in range(4):
                    v.wait_ge(att1.proj, at(i, 3, 1))
                    last = ts(QT[:, t, :], bank(t // 2)[:, t % 2, :], W["qb1"][:, t:t + 1], hmq[:, t:t + 1],
                              ALU.add, ALU.mult)
                last.then_inc(att1.vevac, 1)
                v.wait_ge(att1.proj, at(i, 3, 2))
                for g in range(4):
                    for t in (2, 3):
                        ts(KT16[:, 4 * g + t, :], bank(3)[:, t % 2, :], hmk[:, g, t:t + 1], kbh[:, g, t:t + 1],
                           ALU.mult, ALU.add)
                v.wait_ge(att1.proj, at(i, 3, 3))
                c.link(tt_(ckvT2, bank(4), bc(W["vb1"][:]), ALU.add))
                nc.vector.memset(VP[:, :, :, 16:32], 0.0)
                for t in range(TT):
                    last = tt_(VP[:, t, :, 0:16], ckvT2[:, t, :].rearrange("p (h d) -> p h d", d=16),
                               W["hmv1"][:].rearrange("p (h d) -> p h d", d=16), ALU.mult)
                last.then_inc(att1.vevac, 1)
                attention(i, c, att1)
                c.link(tt_(x[:], x[:], bc(W["ob1"][:]), ALU.add))
                residual(i, c, 4, 2, x[:], None, None)
                normalised(i, c, 6, res, x, D).then_inc(x_ready, 1)
                for n in range(4):
                    v.wait_ge(att2.proj, at(i, 12, n + 1))
                    ts(QT[:, 2 * n:2 * n + 2, :], bank((0, 1, 2, 7)[n]), 0.125, None, ALU.mult).then_inc(att2.vevac, 1)
                for n in range(4):
                    v.wait_ge(att2.proj, at(i, 12, n + 9))
                    cp(VV[:, n // 2, n % 2 * 512:(n % 2 + 1) * 512], ps[:, (0, 1, 2, 7)[n], :]).then_inc(att2.vevac, 1)
                attention(i, c, att2)
                c.link(tt_(x[:], x[:], bc(W["ob2"][:]), ALU.add))
                residual(i, c, 5, 2, x[:], None, None)
                normalised(i, c, 7, res, x, D).then_inc(x_ready, 1)
                moe(i, c)
                residual(i, c, 6, 0, x[:], None, None)
                v.wait_ge(stored, at(i, 16, 16))
                normalised(i, c, 8, res, x_out, D).then_inc(batch_done, 1)
                c.close()


def layouts(a):
    n = {k: np.asarray(v) for k, v in a.items()}

    def tiles(w):
        return np.ascontiguousarray(w.reshape(-1, P, w.shape[1]).transpose(1, 0, 2))

    def columns(w):
        return np.ascontiguousarray(w.reshape(-1, P).T)

    def rows(w):
        return np.ascontiguousarray(np.broadcast_to(w.reshape(1, -1), (P, w.size)))

    def heads16(w):
        o = np.zeros((w.shape[0], 4, 4, 32), w.dtype)
        o[:, :, :, 0:16] = w.reshape(-1, 4, 4, 16).transpose(0, 2, 1, 3)
        return o.reshape(w.shape[0], 512)

    def pad32(w):
        o = np.zeros((H, 32, w.shape[1]), w.dtype)
        o[:, 0:16] = w.reshape(H, 16, -1)
        return pairs(o.reshape(H * 32, -1))

    def pairs(w):
        return w.reshape(2, H // 2, -1, w.shape[1]).transpose(1, 0, 2, 3).reshape(w.shape)

    def heads64(w):
        return w.reshape(-1, 2, 8, 64).transpose(0, 2, 1, 3).reshape(-1, 1024)

    x = n["x"]
    wx = n["L0_attn_W_xproj"]
    qkv = n["L1_attn_qkv_w"].reshape(H, 3, 16, D)
    qkvb = n["L1_attn_qkv_b"].reshape(H, 3, 16)
    hm = np.repeat(n["L1_attn_head_mask"], 16)
    per_head = lambda w: columns(heads16(w.reshape(1, -1)).reshape(-1))
    kup = n["L0_xattn_W_kv_up"]
    experts = lambda w: w.transpose(1, 0, 2).reshape(D, E * FE)
    sel = np.zeros((96, 32), np.float32)
    for r in range(3):
        sel[32 * r + np.arange(32), np.arange(32)] = 1
    bf = np.dtype(mybir.dt.np(BF16))
    tri = np.zeros((P, E, E), np.float32)
    for e in range(E):
        tri[:, e, :e] = 1
    return {
        "x": x.reshape(B, TT, P, D),
        "xT": np.ascontiguousarray(x.transpose(0, 2, 1)).reshape(B, KD, P, T),
        "ctxT": np.ascontiguousarray(n["ctx_1024"].transpose(0, 2, 1)).reshape(B, KD, P, T),
        "idx": np.ascontiguousarray(n["itok_BxSx64_0_2047"].reshape(B, TT, P, SEL).transpose(0, 1, 3, 2)).reshape(B, P, P),
        "w1": tiles(n["L0_ffn_w1"].T), "w2": tiles(n["L0_ffn_w2"].T),
        "win": tiles(n["L0_attn_W_in"]), "wxd": tiles(wx[:, :RANK]),
        "wbc": tiles(np.concatenate([wx[:, RANK:]] * 3, 1)),
        "wdt": n["L0_attn_W_dt"], "wout": tiles(n["L0_attn_W_out"]),
        "convw": tiles(n["L0_attn_conv_w"]), "convb": columns(n["L0_attn_conv_b"]),
        "bdt": columns(n["L0_attn_b_dt"]), "alog": tiles(n["L0_attn_A_log"]), "dp": columns(n["L0_attn_Dp"]),
        "ident": np.eye(P, dtype=np.float32), "identb": np.eye(P, dtype=np.float32).astype(bf), "sel": sel.astype(bf),
        "iota": np.tile(np.arange(32, dtype=np.float32), (P, 1)).astype(bf),
        "group": np.repeat(np.eye(4, dtype=np.float32), 32, 0), "side": np.repeat(np.eye(2, dtype=np.float32), 64, 0),
        "half": np.repeat(np.float32([0, 16]), SEL).reshape(P, 1), "ones": np.ones((P, P), np.float32), "tri": tri,
        "wq0": tiles(heads16(n["L0_xattn_W_q"].T)), "wdown0": tiles(n["L0_xattn_W_kv_down"].T),
        "wk0": heads16(kup[:D].T), "wv0": np.ascontiguousarray(kup[D:].T), "wo0": tiles(pad32(n["L0_xattn_W_out"].T)),
        "ln1g": rows(n["L0_ffn_ln1_g"]), "ln1b": rows(n["L0_ffn_ln1_b"]), "fb1": rows(n["L0_ffn_b1"]),
        "ln2g": rows(n["L0_ffn_ln2_g"]), "ln2b": rows(n["L0_ffn_ln2_b"]), "fb2": rows(n["L0_ffn_b2"]),
        "wq1": tiles(heads16(qkv[:, 0].reshape(D, D).T)), "wk1": tiles(heads16(qkv[:, 1].reshape(D, D).T)),
        "wv1": tiles(qkv[:, 2].reshape(D, D).T),
        "qb1": per_head(qkvb[:, 0]), "kb1": per_head(qkvb[:, 1]), "hm1": per_head(hm),
        "vb1": rows(qkvb[:, 2]), "hmv1": rows(hm),
        "wo1": tiles(pad32(n["L1_attn_fc_w"].T)), "ob1": rows(n["L1_attn_fc_b"]),
        "wq2": tiles(heads64(n["L1_xattn_Wq"])), "wk2": tiles(heads64(n["L1_xattn_Wkv"][:, :1024])),
        "wv2": tiles(n["L1_xattn_Wkv"][:, 1024:]), "wo2": tiles(pairs(n["L1_xattn_Wo"])), "ob2": rows(n["L1_xattn_bo"]),
        "router": tiles(n["L1_ffn_router_w"]),
        "wgate": tiles(np.concatenate([experts(n["L1_ffn_w_gate"]), n["L1_ffn_ws_gate"]], 1)),
        "wup": tiles(np.concatenate([experts(n["L1_ffn_w_up"]), n["L1_ffn_ws_up"]], 1)),
        "wmoe": tiles(np.concatenate([n["L1_ffn_w_down"].reshape(E * FE, D), n["L1_ffn_ws_down"]], 0)),
    }


def kernel(**inputs):
    from concourse import bacc
    from concourse.bass_utils import run_bass_kernel_spmd

    nc = bacc.Bacc("TRN2", target_bir_lowering=False, num_devices=1)
    arrays, dram = {}, {}
    for name, a in layouts(inputs).items():
        a = np.ascontiguousarray(a)
        arrays[f"in_{name}"] = a
        dram[name] = nc.dram_tensor(f"in_{name}", a.shape, mybir.dt.from_np(a.dtype), kind="ExternalInput").ap()
    out = nc.dram_tensor("out_x", (B, TT, P, D), F32, kind="ExternalOutput").ap()
    build(nc, dram, out)
    r = run_bass_kernel_spmd(nc, [arrays], core_ids=[0])
    return r.results[0]["out_x"].reshape(B, T, D)
```
